# Optimizing a Trainium2 kernel written in Bass

```python
import numpy as np
import jax
import jax.numpy as jnp

def _softmax(x, axis=-1):
    return jax.nn.softmax(x, axis=axis)

def _gelu(x):
    return jax.nn.gelu(x, approximate=True)

def _silu(x):
    return jax.nn.silu(x)

def _sigmoid(x):
    return jax.nn.sigmoid(x)

def _layernorm(x, axis=-1, eps=1e-05):
    m = jnp.mean(x, axis=axis, keepdims=True)
    v = jnp.var(x, axis=axis, keepdims=True)
    return (x - m) / jnp.sqrt(v + eps)

def _scatter_add(tgt, idx, src, axis=0):
    return tgt.at[idx].add(src)

def _segment_sum(src, seg, n):
    return jax.ops.segment_sum(src, seg, n)
kernel_name = 'mk_recurrent_d2_jaxref_r8_4292d5'

def setup_inputs(seed: int=0):
    np.random.seed(seed)
    _w = jnp.asarray

    def _L0_attn_setup():
        import jax, jax.numpy as jnp
        import numpy as np
        N_HEADS = 16
        INPUT_DIM = 128
        EMBED_DIM = 128
        KEY_DIM = EMBED_DIM // N_HEADS
        BATCH = 4
        SEQ = 256

        def _uniform(key, shape, bound):
            return jax.random.uniform(key, shape, jnp.float32, -bound, bound)
        key = jax.random.key(seed)
        kq, k1, k2, k3, k4 = jax.random.split(key, 5)
        stdv_k = 1.0 / np.sqrt(KEY_DIM)
        stdv_e = 1.0 / np.sqrt(EMBED_DIM)
        return {'q': jax.random.normal(kq, (BATCH, SEQ, INPUT_DIM), jnp.float32), 'W_query': _uniform(k1, (N_HEADS, INPUT_DIM, KEY_DIM), stdv_k), 'W_key': _uniform(k2, (N_HEADS, INPUT_DIM, KEY_DIM), stdv_k), 'W_val': _uniform(k3, (N_HEADS, INPUT_DIM, KEY_DIM), stdv_k), 'W_out': _uniform(k4, (N_HEADS, KEY_DIM, EMBED_DIM), stdv_e)}
    _L0_attn_in = _L0_attn_setup()

    def _L0_ffn_setup():
        import jax, jax.numpy as jnp
        import numpy as np
        LOOPS = 2
        NUM_GROUPS = 4
        EXPERTS_PER_GROUP = 2
        NUM_EXPERTS = NUM_GROUPS * EXPERTS_PER_GROUP
        GROUPS_TOP_K = 2
        TOP_K = 1
        RMS_EPS = 1e-06
        EPS = 1e-09

        def _rmsnorm(x, w):
            return x * jax.lax.rsqrt(jnp.mean(x * x, axis=-1, keepdims=True) + RMS_EPS) * w

        def _combine_weights(x_flat, w_macro, w_micro):
            T = x_flat.shape[0]
            macro = jax.nn.softmax(x_flat @ w_macro.T, axis=-1)
            mvals, midx = jax.lax.top_k(macro, GROUPS_TOP_K)
            mvals = mvals / (jnp.sum(mvals, axis=-1, keepdims=True) + EPS)
            micro = jax.nn.softmax(jnp.einsum('td,ged->tge', x_flat, w_micro), axis=-1)
            uvals, uidx = jax.lax.top_k(micro, TOP_K)
            uvals = uvals / (jnp.sum(uvals, axis=-1, keepdims=True) + EPS)
            tok = jnp.arange(T)
            combine = jnp.zeros((T, NUM_EXPERTS), x_flat.dtype)
            for s in range(GROUPS_TOP_K):
                g = midx[:, s]
                wg = mvals[:, s:s + 1]
                li = uidx[tok, g]
                lv = uvals[tok, g]
                eidx = g[:, None] * EXPERTS_PER_GROUP + li
                combine = combine.at[tok[:, None], eidx].add(lv * wg)
            return combine
        key = jax.random.key(seed)
        ks = jax.random.split(key, 6)
        B, S, D, F = (2, 128, 128, 256)
        return {'z': jax.random.normal(ks[0], (B, S, D), jnp.float32), 'norm_w': jnp.ones((D,), jnp.float32), 'w_macro': jax.random.normal(ks[1], (NUM_GROUPS, D), jnp.float32) * D ** (-0.5), 'w_micro': jax.random.normal(ks[2], (NUM_GROUPS, EXPERTS_PER_GROUP, D), jnp.float32) * D ** (-0.5), 'w1': jax.random.normal(ks[3], (NUM_EXPERTS, F, D), jnp.float32) * D ** (-0.5), 'w2': jax.random.normal(ks[4], (NUM_EXPERTS, D, F), jnp.float32) * F ** (-0.5)}
    _L0_ffn_in = _L0_ffn_setup()

    def _L1_attn_setup():
        import jax, jax.numpy as jnp
        import numpy as np
        DIM = 128
        B, S = (4, 512)
        key = jax.random.key(seed)
        ks = jax.random.split(key, 12)
        d = DIM

        def lin(k, out_d, in_d):
            bound = 1.0 / np.sqrt(in_d)
            kw, kb = jax.random.split(k)
            W = jax.random.uniform(kw, (out_d, in_d), jnp.float32, -bound, bound)
            b = jax.random.uniform(kb, (out_d,), jnp.float32, -bound, bound)
            return (W, b)
        x = jax.random.normal(ks[0], (B, S, d), jnp.float32)
        random_phases = jax.random.normal(ks[1], (d,), jnp.float32) * (2.0 * np.pi)
        W_mag, b_mag = lin(ks[2], d, d)
        W_q, b_q = lin(ks[3], d, d)
        ln_g = jnp.ones((4 * d,), jnp.float32)
        ln_b = jnp.zeros((4 * d,), jnp.float32)
        W1, b1 = lin(ks[4], 2 * d, 4 * d)
        W2, b2 = lin(ks[5], d, 2 * d)
        return {'x': x, 'random_phases': random_phases, 'W_mag': W_mag, 'b_mag': b_mag, 'W_q': W_q, 'b_q': b_q, 'ln_g': ln_g, 'ln_b': ln_b, 'W1': W1, 'b1': b1, 'W2': W2, 'b2': b2}
    _L1_attn_in = _L1_attn_setup()

    def _L1_ffn_setup():
        import jax, jax.numpy as jnp
        import numpy as np
        TOP_K = 2
        key = jax.random.key(seed)
        k1, k2, k3, k4 = jax.random.split(key, 4)
        B, S, D = (2, 256, 128)
        E, W = (8, 128)
        x = jax.random.normal(k1, (B, S, D), dtype=jnp.float32)
        router_w = jax.random.normal(k2, (E, D), dtype=jnp.float32) * 0.02
        w1 = jax.random.normal(k3, (D, E * W), dtype=jnp.float32) * 0.02
        w2 = jax.random.normal(k4, (E * W, D), dtype=jnp.float32) * 0.02
        return {'x': x, 'router_w': router_w, 'w1': w1, 'w2': w2}
    _L1_ffn_in = _L1_ffn_setup()
    _d = {'L0_attn_q': _L0_attn_in['q'], 'L0_attn_W_query': _L0_attn_in['W_query'], 'L0_attn_W_key': _L0_attn_in['W_key'], 'L0_attn_W_val': _L0_attn_in['W_val'], 'L0_attn_W_out': _L0_attn_in['W_out'], 'L0_ffn_norm_w': _L0_ffn_in['norm_w'], 'L0_ffn_w_macro': _L0_ffn_in['w_macro'], 'L0_ffn_w_micro': _L0_ffn_in['w_micro'], 'L0_ffn_w1': _L0_ffn_in['w1'], 'L0_ffn_w2': _L0_ffn_in['w2'], 'L1_attn_random_phases': _L1_attn_in['random_phases'], 'L1_attn_W_mag': _L1_attn_in['W_mag'], 'L1_attn_b_mag': _L1_attn_in['b_mag'], 'L1_attn_W_q': _L1_attn_in['W_q'], 'L1_attn_b_q': _L1_attn_in['b_q'], 'L1_attn_ln_g': _L1_attn_in['ln_g'], 'L1_attn_ln_b': _L1_attn_in['ln_b'], 'L1_attn_W1': _L1_attn_in['W1'], 'L1_attn_b1': _L1_attn_in['b1'], 'L1_attn_W2': _L1_attn_in['W2'], 'L1_attn_b2': _L1_attn_in['b2'], 'L1_ffn_router_w': _L1_ffn_in['router_w'], 'L1_ffn_w1': _L1_ffn_in['w1'], 'L1_ffn_w2': _L1_ffn_in['w2']}
    _x0 = _d['L0_attn_q']
    _d['L0_attn_q'] = jax.random.normal(jax.random.fold_in(jax.random.key(seed), 1), (8, 512, 128), dtype=_x0.dtype)
    del _x0
    return _d

def reference(L0_attn_q, L0_attn_W_query, L0_attn_W_key, L0_attn_W_val, L0_attn_W_out, L0_ffn_norm_w, L0_ffn_w_macro, L0_ffn_w_micro, L0_ffn_w1, L0_ffn_w2, L1_attn_random_phases, L1_attn_W_mag, L1_attn_b_mag, L1_attn_W_q, L1_attn_b_q, L1_attn_ln_g, L1_attn_ln_b, L1_attn_W1, L1_attn_b1, L1_attn_W2, L1_attn_b2, L1_ffn_router_w, L1_ffn_w1, L1_ffn_w2):

    def _L0_attn_ref(q, W_query, W_key, W_val, W_out):
        import jax, jax.numpy as jnp
        import numpy as np
        N_HEADS = 16
        INPUT_DIM = 128
        EMBED_DIM = 128
        KEY_DIM = EMBED_DIM // N_HEADS
        BATCH = 4
        SEQ = 256

        def _uniform(key, shape, bound):
            return jax.random.uniform(key, shape, jnp.float32, -bound, bound)
        norm = 1.0 / np.sqrt(KEY_DIM)
        Q = jnp.einsum('bsd,hdk->hbsk', q, W_query)
        K = jnp.einsum('bsd,hdk->hbsk', q, W_key)
        V = jnp.einsum('bsd,hdv->hbsv', q, W_val)
        scores = norm * jnp.einsum('hbqk,hbnk->hbqn', Q, K)
        attn = jax.nn.softmax(scores, axis=-1)
        heads = jnp.einsum('hbqn,hbnv->hbqv', attn, V)
        out = jnp.einsum('hbqv,hve->bqe', heads, W_out)
        return out

    def _L0_ffn_ref(z, norm_w, w_macro, w_micro, w1, w2):
        import jax, jax.numpy as jnp
        import numpy as np
        LOOPS = 2
        NUM_GROUPS = 4
        EXPERTS_PER_GROUP = 2
        NUM_EXPERTS = NUM_GROUPS * EXPERTS_PER_GROUP
        GROUPS_TOP_K = 2
        TOP_K = 1
        RMS_EPS = 1e-06
        EPS = 1e-09

        def _rmsnorm(x, w):
            return x * jax.lax.rsqrt(jnp.mean(x * x, axis=-1, keepdims=True) + RMS_EPS) * w

        def _combine_weights(x_flat, w_macro, w_micro):
            T = x_flat.shape[0]
            macro = jax.nn.softmax(x_flat @ w_macro.T, axis=-1)
            mvals, midx = jax.lax.top_k(macro, GROUPS_TOP_K)
            mvals = mvals / (jnp.sum(mvals, axis=-1, keepdims=True) + EPS)
            micro = jax.nn.softmax(jnp.einsum('td,ged->tge', x_flat, w_micro), axis=-1)
            uvals, uidx = jax.lax.top_k(micro, TOP_K)
            uvals = uvals / (jnp.sum(uvals, axis=-1, keepdims=True) + EPS)
            tok = jnp.arange(T)
            combine = jnp.zeros((T, NUM_EXPERTS), x_flat.dtype)
            for s in range(GROUPS_TOP_K):
                g = midx[:, s]
                wg = mvals[:, s:s + 1]
                li = uidx[tok, g]
                lv = uvals[tok, g]
                eidx = g[:, None] * EXPERTS_PER_GROUP + li
                combine = combine.at[tok[:, None], eidx].add(lv * wg)
            return combine
        B, S, D = z.shape
        T = B * S
        for _ in range(LOOPS):
            zn = _rmsnorm(z, norm_w)
            x = zn.reshape(T, D)
            combine = _combine_weights(x, w_macro, w_micro)
            h = jax.nn.silu(jnp.einsum('td,efd->tef', x, w1))
            y = jnp.einsum('tef,edf->ted', h, w2)
            mixed = jnp.einsum('ted,te->td', y, combine)
            z = z + mixed.reshape(B, S, D)
        return z

    def _L1_attn_ref(x, random_phases, W_mag, b_mag, W_q, b_q, ln_g, ln_b, W1, b1, W2, b2):
        import jax, jax.numpy as jnp
        import numpy as np
        DIM = 128
        B, S = (4, 512)
        Bx, Sx, D = x.shape
        magnitude = jax.nn.sigmoid(jnp.einsum('bsd,ed->bse', x, W_mag) + b_mag) * 5.0
        position = jnp.arange(Sx, dtype=x.dtype)[None, :, None]
        phi = random_phases[None, None, :] * position * 0.01
        cos_phi = jnp.cos(phi)
        sin_phi = jnp.sin(phi)
        weighted = magnitude * x
        mem_r = jnp.cumsum(weighted * cos_phi, axis=1)
        mem_i = jnp.cumsum(weighted * sin_phi, axis=1)
        acc_mag = jnp.cumsum(magnitude, axis=1)
        inv_sqrt = 1.0 / jnp.sqrt(acc_mag + 1e-08)
        mr = mem_r * inv_sqrt
        mi = mem_i * inv_sqrt
        q_off = jnp.einsum('bsd,ed->bse', x, W_q) + b_q
        phi_q = phi + q_off
        cq = jnp.cos(phi_q)
        sq = jnp.sin(phi_q)
        retrieved_r = mr * cq + mi * sq
        retrieved_i = mi * cq - mr * sq
        context = jnp.concatenate([x * cos_phi, x * sin_phi, retrieved_r, retrieved_i], axis=-1)
        mu = jnp.mean(context, axis=-1, keepdims=True)
        var = jnp.mean((context - mu) ** 2, axis=-1, keepdims=True)
        h = (context - mu) / jnp.sqrt(var + 1e-05) * ln_g + ln_b
        h = jax.nn.gelu(jnp.einsum('bsf,gf->bsg', h, W1) + b1, approximate=False)
        out = jnp.einsum('bsg,dg->bsd', h, W2) + b2
        return x + out

    def _L1_ffn_ref(x, router_w, w1, w2):
        import jax, jax.numpy as jnp
        import numpy as np
        TOP_K = 2
        B, S, D = x.shape
        E = router_w.shape[0]
        W = w1.shape[1] // E
        T = B * S
        xf = x.reshape(T, D)
        router_logits = jnp.einsum('td,ed->te', xf, router_w)
        router_probs = jax.nn.sigmoid(router_logits.astype(jnp.float32))
        top_w, sel = jax.lax.top_k(router_probs, TOP_K)
        top_w = top_w / (top_w.sum(axis=-1, keepdims=True) + 1e-20)
        top_w = top_w.astype(x.dtype)
        W1e = w1.reshape(D, E, W).transpose(1, 0, 2)
        W2e = w2.reshape(E, W, D)
        h = jnp.einsum('td,edw->etw', xf, W1e)
        a = jnp.square(jax.nn.relu(h))
        y = jnp.einsum('etw,ewd->etd', a, W2e)
        cw = jnp.zeros((T, E), dtype=x.dtype).at[jnp.arange(T)[:, None], sel].set(top_w)
        out = jnp.einsum('etd,te->td', y, cw)
        return out.reshape(B, S, D)
    x = L0_attn_q
    xn = _layernorm(x, axis=-1)
    s = _L0_attn_ref(xn, L0_attn_W_query, L0_attn_W_key, L0_attn_W_val, L0_attn_W_out)
    g = _silu(_L0_ffn_ref(xn, L0_ffn_norm_w, L0_ffn_w_macro, L0_ffn_w_micro, L0_ffn_w1, L0_ffn_w2))
    x = x + s * g
    xn = _layernorm(x, axis=-1)
    s = _L1_attn_ref(xn, L1_attn_random_phases, L1_attn_W_mag, L1_attn_b_mag, L1_attn_W_q, L1_attn_b_q, L1_attn_ln_g, L1_attn_ln_b, L1_attn_W1, L1_attn_b1, L1_attn_W2, L1_attn_b2)
    g = _silu(_L1_ffn_ref(xn, L1_ffn_router_w, L1_ffn_w1, L1_ffn_w2))
    x = x + s * g
    return x

_drawn_inputs = setup_inputs


def setup_inputs(seed=0):
    import zlib

    import numpy as np

    out = dict(_drawn_inputs(seed))
    spreads = {'L0_ffn_norm_w': (1.0, 0.2), 'L1_attn_ln_g': (1.0, 0.6), 'L1_attn_ln_b': (0.0, 0.8)}
    factors = {'L1_attn_random_phases': 8.0,
     'L1_attn_W_mag': 8.0,
     'L1_attn_b_mag': 8.0,
     'L1_attn_W_q': 8.0,
     'L1_attn_b_q': 8.0,
     'L1_attn_W1': 8.0,
     'L1_attn_b1': 8.0,
     'L1_attn_W2': 8.0,
     'L1_attn_b2': 37.257,
     'L1_ffn_router_w': 8.0,
     'L1_ffn_w1': 8.0,
     'L1_ffn_w2': 8.0}
    for name, (base, spread) in spreads.items():
        noise = np.random.default_rng([zlib.crc32(name.encode()), seed]).standard_normal(out[name].shape)
        drawn = base * np.exp(spread * noise) if base else spread * noise
        out[name] = jnp.asarray(drawn.astype(out[name].dtype))
    for name, factor in factors.items():
        out[name] = (out[name] * factor).astype(out[name].dtype)
    return out
```

```python
from contextlib import ExitStack

import numpy as np

import concourse.bass as bass
from concourse import mybir

F32 = mybir.dt.float32
F32R = mybir.dt.float32r
BF16 = mybir.dt.bfloat16
ALU = mybir.AluOpType
ACT = mybir.ActivationFunctionType
AX = mybir.AxisListType

P = 128
B, S, D = 8, 512, 128
NT = S // P
H, HD = 16, 8
HJ = H // 2
PIECES = 3
Q_PART = (0, 0, 0, 1, 1, 2)
K_PART = (0, 1, 2, 0, 1, 0)
ROWS = len(Q_PART) * HD
E0, F0 = 8, 256
C0 = E0 * F0 // P
LOOPS = 2
GROUPS = 4
E1 = 8
G1 = 2 * D
CTX = 4
ROUND = float(1.5 * 2 ** 23)
TWO_PI_A = 6.28125
TWO_PI_B = float(2 * np.pi - 6.28125)
PI_BELOW = 3.1415925
MAG = 2.5

FIRST = dict(ident=128, wq=128, wk=128, wv=128, wr=GROUPS + E0, norm_w=1, phases=1, b_mag=1, b_q=1,
             ln_g=CTX, ln_b=CTX, lower=128, pos=S)
SECOND = dict(wo=128, w_mag=128, w_q=128, w2m=G1, wr1=E1, w1m=CTX * G1)


def columns(widths, name):
    at = 0
    for n, w in widths.items():
        if n == name:
            return slice(at, at + w)
        at += w


def build(nc, x, first, second, w1, w2, v1, v2, rows, select, out):
    ctx = ExitStack()
    with ctx:
        def sb(name, shape, dt=F32):
            return ctx.enter_context(nc.sbuf_tensor(name, shape, dt))

        def psum(name, shape, dt=F32):
            return ctx.enter_context(nc.psum_tensor(name, shape, dt))

        c_first = sb("c_first", [P, sum(FIRST.values())])
        c_second = sb("c_second", [P, sum(SECOND.values())])

        def f_(name):
            return c_first[:, columns(FIRST, name)]

        def g_(name):
            return c_second[:, columns(SECOND, name)]

        ident, wq, wk, wv, wr = f_("ident"), f_("wq"), f_("wk"), f_("wv"), f_("wr")
        lower = f_("lower")
        wo, w_mag, w_q, wr1 = g_("wo"), g_("w_mag"), g_("w_q"), g_("wr1")
        w2m = g_("w2m").rearrange("p (c d) -> p c d", c=2)
        w1m = g_("w1m").rearrange("p (c g) -> p c g", c=CTX)
        w1_hi, w1_lo = sb("w1_hi", [P, C0 * P], F32R), sb("w1_lo", [P, C0 * P], F32R)
        v1_hi, v1_lo = sb("v1_hi", [P, E1 * P], F32R), sb("v1_lo", [P, E1 * P], F32R)
        w2_sb, v2_sb = sb("w2_sb", [P, C0, D]), sb("v2_sb", [P, E1, D])
        rows_sb = sb("rows_sb", [1, G1 + D])
        select_sb = sb("select_sb", [PIECES * E0, E0 * P], BF16)
        select_v = select_sb[:, :].rearrange("k (e p) -> k e p", e=E0)
        ident_b = sb("ident_b", [P, P], BF16)
        ones = sb("ones", [P, P])
        ones_row = sb("ones_row", [P, S])
        mean_col = sb("mean_col", [P, 1])
        half_pi = sb("half_pi", [P, 1])
        tiny = sb("tiny", [P, 1])
        b_mag_half = sb("b_mag_half", [P, 1])
        minus_half = sb("minus_half", [P, NT])
        euler = sb("euler", [P, NT * E1])
        phi, cos_phi, sin_phi = sb("phi", [P, S]), sb("cos_phi", [P, S]), sb("sin_phi", [P, S])
        w1g = sb("w1g", [P, CTX, G1])
        w1_sums, b1_all = sb("w1_sums", [P, G1]), sb("b1_all", [P, G1])

        xin = sb("xin", [P, NT, D])
        z = sb("z", [P, NT, D])
        zs = sb("zs", [P, NT, D])
        bn6, mv = sb("bn6", [P, NT, 6]), sb("mv", [P, NT, 2])
        ssq, rstd = sb("ssq", [P, NT]), sb("rstd", [P, NT])
        xT = sb("xT", [P, S])
        x_hi, x_lo = sb("x_hi", [P, S], F32R), sb("x_lo", [P, S], F32R)
        parts = sb("parts", [P, 2, PIECES, S], BF16)
        rest = sb("rest", [P, 2, S])
        q_st, k_st = sb("q_st", [P, HJ, S], BF16), sb("k_st", [P, HJ, S], BF16)
        v_aug = sb("v_aug", [P, NT * H, 32])
        hid = sb("hid", [P, C0, S])
        cb = sb("cb", [P, E0, S])
        ct = sb("ct", [PIECES * E0, S], BF16)
        cp = sb("cp", [P, NT, PIECES * E0], BF16)
        yT = sb("yT", [P, S])
        smax = sb("smax", [P, NT, H])
        mrest = sb("mrest", [P, NT, H])
        mp = sb("mp", [P, NT, PIECES * H], BF16)
        mpt = sb("mpt", [PIECES * H, S], BF16)
        probs = sb("probs", [P, 2, 4, S])
        o_sb = sb("o_sb", [P, S])
        oden = sb("oden", [P, NT * 4, 1])
        on = sb("on", [P, NT, 4, 32])
        hT = sb("hT", [P, S])
        gate = sb("gate", [P, S])
        x1 = sb("x1", [P, NT, D])
        outb = sb("outb", [P, NT, D])
        lg = sb("lg", [P, NT, 12])
        lm = sb("lm", [P, NT, 5])
        le = sb("le", [P, NT, 12])
        ld = sb("ld", [P, NT, 12])
        lt = sb("lt", [P, NT, 12])
        beat, tie = sb("beat", [P, NT * 8 * 8]), sb("tie", [P, NT * 8 * 8])
        rank = sb("rank", [P, NT * 8])
        cw = sb("cw", [P, NT, E0])
        crest = sb("crest", [P, NT, E0])
        wsum = sb("wsum", [P, NT])
        gw = sb("gw", [P, NT, GROUPS])
        tg, wgt, turns, phq = (probs[:, 0, n, :] for n in range(4))
        ph_abs, cq, sq, wc = (probs[:, 1, n, :] for n in range(4))
        mem_r, mem_i = rest[:, 0, :], rest[:, 1, :]
        ctxt, ctx2 = hid[:, 8:12, :], hid[:, 12:16, :]
        ws, acc, inv = sb("ws", [P, S]), sb("acc", [P, S]), sb("inv", [P, S])
        stat = sb("stat", [P, NT, 2])
        var = sb("var", [P, NT])
        nmr = sb("nmr", [P, NT])
        gb, ga = (cb[:, n:n + 2, :].rearrange("p a (t g) -> p (a t) g", t=2) for n in (0, 2))
        gT = cb[:, 4:6, :]
        yn = sb("yn", [P, NT, D])

        scr_q = nc.dram_tensor("scr_q", [2, len(Q_PART), HD * HJ, S], BF16).ap()
        scr_k = nc.dram_tensor("scr_k", [2, len(K_PART), HD * HJ, S], BF16).ap()
        scr_m = nc.dram_tensor("scr_m", [PIECES, 2, HJ, S], BF16).ap()

        ps_s = psum("ps_s", [P, 4, S])
        ps_u = psum("ps_u", [P, 2, S])
        ps_y = psum("ps_y", [P, S])
        ps_m = psum("ps_m", [P, S])
        ps_m16 = ps_m[:, :].bitcast(BF16)

        def sem(name):
            return ctx.enter_context(nc.semaphore(name))

        first_in, second_in, v_in = sem("first_in"), sem("second_in"), sem("v_in")
        w_in = sem("w_in")
        x_in, stored = sem("x_in"), sem("stored")
        set_up = sem("set_up")
        set_pool, set_pe, set_act = sem("set_pool"), sem("set_pe"), sem("set_act")
        met = sem("met")
        go = {n: sem(f"go_{n}") for n in ("pe", "act", "dve", "pool")}

        body = {}

        for name in (
            "stats0 rstd_ok z_ok zT_ps xnT_ok qkv_ps part_ok rest_ok parts_ok v_ok q_out k_out stack_ok "
            "ssq_ok zs_ok xT_ok hi_ok lo_ok lg_ps lt_in lt_ok cp_ok ct_ps ct_ok cb_ps cb_ok u_ps h_ok hc_ok "
            "y_ps yT_ok yN_ps s1_ps max_ok mp_ok mpt_ps mpt_ok m_out shift_ok s2_ps p_ok pv_ps o_ok oN_ps "
            "on_ok onT_ps hT_ok att_ps gate_ok x1_ok mq_ps tg_ok ph_ok sc_ok acc_ok inv_in mem_ok f_ps r_ok "
            "a_ok sg_in sg_ok mul_ok c01_ok rot_in ri_ok sq_ok st_ps var_ok g_ps ga_ok ge_ok gT_ps gT_ok "
            "mlp_ps out_ok dve pool"
        ).split():
            body[name] = sem(name)
        numbers = sorted(int(s.num) for s in body.values())
        assert numbers[-1] - numbers[0] == len(numbers) - 1
        w = type("W", (), body)

        UNITS = 2 * H
        after = {}
        for n in range(UNITS):
            if n < 16:
                at = (0, 16 + n)
            else:
                at = (1, 5 + (n - 16) * 11 // 16)
            after.setdefault(at, []).append(n)

        block = ctx.enter_context(nc.Block())

        @block.sync
        def _(e):
            def load_x(b):
                e.dma_start(xin[:, :, :], x[bass.ds(b, 1)].rearrange("o (t p) d -> p (o t) d", p=P)
                            ).then_inc(x_in, 16)

            load_x(0)
            e.dma_start(c_first[:, :], first).then_inc(first_in, 16)
            e.dma_start(hid[:, 0:4, :], w1.rearrange("p (a n) -> p a n", a=4)).then_inc(w_in, 16)
            e.dma_start(hid[:, 4:6, :], v1.rearrange("p (a n) -> p a n", a=2)).then_inc(w_in, 16)
            e.dma_start(hid[0:PIECES * E0, 6:8, :], select.rearrange("p (a n) -> p a n", a=2)).then_inc(w_in, 16)
            e.dma_start(w2_sb[:, :, :], w2.rearrange("p (c d) -> p c d", c=C0)).then_inc(v_in, 16)
            e.dma_start(c_second[:, :], second).then_inc(second_in, 16)
            e.dma_start(rows_sb[:, :], rows).then_inc(second_in, 16)
            e.dma_start(v2_sb[:, :, :], v2.rearrange("p (c d) -> p c d", c=E1)).then_inc(v_in, 16)
            with e.Fori(0, B) as b:
                for which, scr, pattern, out_sem in ((0, scr_q, Q_PART, w.q_out), (1, scr_k, K_PART, w.k_out)):
                    e.wait_ge(w.parts_ok, which + 1)
                    for half in range(2):
                        for c, part in enumerate(pattern):
                            e.dma_start(scr[half, c],
                                        parts[64 * half:64 * half + 64, which, part, :]).then_inc(out_sem, 16)
                for scr, dst, out_sem in ((scr_q, q_st, w.q_out), (scr_k, k_st, w.k_out)):
                    e.wait_ge(out_sem, 16 * 2 * len(Q_PART))
                    for half in range(2):
                        e.dma_start(dst[64 * half:64 * half + ROWS, :, :],
                                    scr[half].rearrange("c (k j) n -> (c k) j n", j=HJ)).then_inc(w.stack_ok, 16)
                e.wait_ge(w.mpt_ok, 1)
                e.dma_start(scr_m.rearrange("p h j n -> (p h j) n"), mpt[:, :]).then_inc(w.m_out, 16)
                e.wait_ge(w.m_out, 16)
                for half in range(2):
                    e.dma_start(q_st[64 * half + ROWS:64 * half + ROWS + PIECES, :, :],
                                scr_m[:, half]).then_inc(w.shift_ok, 16)
                e.wait_ge(w.x1_ok, 1)
                load_x((b + 1) & (B - 1))
                e.wait_ge(w.out_ok, 1)
                e.dma_start(out[bass.ds(b, 1)].rearrange("o (t p) d -> p (o t) d", p=P), outb[:, :, :]
                            ).then_inc(stored, 16)
                e.wait_ge(met, 4)
                e.wait_ge(stored, 16)
                e.nop().then_inc(met, -4)
                e.nop().then_inc(stored, -16)
                e.sem_clear(range(numbers[0], numbers[-1] + 1))
                for n in go:
                    e.sem_inc(go[n], 1)
            e.wait_ge(x_in, 16)

        def meet(e, name):
            e.drain().then_inc(met, 1)
            e.wait_ge(go[name], 1)
            e.nop().then_inc(go[name], -1)

        @block.tensor
        def _(e):
            e.wait_ge(set_pe, 1)
            for c in range(CTX):
                i = e.matmul(ps_s[:, 0, 0:G1], ones[:, :], w1g[:, c, :], start=c == 0, stop=c == CTX - 1)
            for c in range(CTX):
                e.matmul(ps_s[:, 1, 0:G1], hid[:, 8, c * P:(c + 1) * P], w1m[:, c, :], start=c == 0, stop=False)
            i = e.matmul(ps_s[:, 1, 0:G1], ones[0:1, :], rows_sb[:, 0:G1], start=False, stop=True)
            i.then_inc(set_act, 1)

            def transposed(src, dst, idt, done):
                for t in range(NT):
                    i = e.transpose(dst(t), src(t), idt)
                i.then_inc(done, 1)

            def unit(n):
                if n >= 2:
                    e.wait_ge(w.max_ok, n - 1)
                else:
                    e.wait_ge(w.stack_ok, 64)
                half, j = n // 2 // HJ, n // 2 % HJ
                for a in range(2):
                    t = 2 * (n % 2) + a
                    i = e.matmul(ps_s[:, 2 * (n % 2) + a, :],
                                 q_st[64 * half:64 * half + ROWS, j, t * P:(t + 1) * P],
                                 k_st[64 * half:64 * half + ROWS, j, :], start=True, stop=True)
                i.then_inc(w.s1_ps, 1)

            def shift_rows():
                e.wait_ge(w.mp_ok, 1)
                transposed(lambda t: mp[:, t, :], lambda t: ps_m16[0:PIECES * H, t * P:(t + 1) * P],
                           ident_b[:, :], w.mpt_ps)

            def choice_rows(n):
                e.wait_ge(w.cp_ok, n)
                transposed(lambda t: cp[:, t, :], lambda t: ps_m16[0:PIECES * E0, t * P:(t + 1) * P],
                           ident_b[:, :], w.ct_ps)

            def choice(n, ex):
                e.wait_ge(w.ct_ok, n)
                if ex:
                    e.wait_ge(w.cb_ok, E0 * (n - 1) + ex)
                e.matmul(ps_m[:, :], select_v[:, ex, :], ct[:, :], start=True, stop=True).then_inc(w.cb_ps, 1)

            with e.Fori(0, B):
                e.wait_ge(w.z_ok, 1)
                transposed(lambda t: z[:, t, :], lambda t: ps_m[:, t * P:(t + 1) * P], ident, w.zT_ps)
                e.wait_ge(w.xnT_ok, 1)
                e.matmul(ps_u[:, 0, :], wq, hT[:, :], start=True, stop=True).then_inc(w.qkv_ps, 1)
                e.matmul(ps_u[:, 1, :], wk, hT[:, :], start=True, stop=True).then_inc(w.qkv_ps, 1)
                for t in range(NT):
                    i = e.matmul(ps_y[:, t * P:(t + 1) * P], hT[:, t * P:(t + 1) * P], wv, start=True, stop=True)
                i.then_inc(w.qkv_ps, 1)

                for loop in range(LOOPS):
                    e.wait_ge(w.zs_ok, loop + 1)
                    if loop:
                        e.wait_ge(w.z_ok, loop + 1)
                    transposed(lambda t: zs[:, t, :], lambda t: ps_m[:, t * P:(t + 1) * P], ident, w.zT_ps)
                    e.wait_ge(w.xT_ok, loop + 1)
                    for t in range(NT):
                        i = e.matmul(ps_m[:, t * 12:(t + 1) * 12], xT[:, t * P:(t + 1) * P], wr,
                                     start=True, stop=True)
                    i.then_inc(w.lg_ps, 1)
                    e.wait_ge(w.hi_ok, loop + 1)
                    for i_ in range(C0):
                        n = C0 * loop + i_
                        if n >= 2:
                            e.wait_ge(w.h_ok, n - 1)
                        else:
                            e.wait_ge(w.rest_ok, n + 1)
                            e.wait_ge(w.part_ok, n + 1)
                        u, cols = ps_u[:, i_ % 2, :], slice(i_ * P, (i_ + 1) * P)
                        e.matmul(u, w1_hi[:, cols], x_hi[:, :], start=True, stop=False)
                        e.matmul(u, w1_lo[:, cols], x_hi[:, :], start=False, stop=False)
                        if i_ == 0:
                            e.wait_ge(w.lo_ok, loop + 1)
                        e.matmul(u, w1_hi[:, cols], x_lo[:, :], start=False, stop=True).then_inc(w.u_ps, 1)
                        for m in after.get((loop, i_), ()):
                            unit(m)
                    choice_rows(loop + 1)
                    choice(loop + 1, 0)
                    for i_ in range(C0):
                        if i_ % 2 and i_ // 2 + 1 < E0:
                            choice(loop + 1, i_ // 2 + 1)
                        e.wait_ge(w.hc_ok, C0 * loop + i_ + 1)
                        if i_ == 0 and loop == 0:
                            e.wait_ge(w.v_ok, 1)
                        i = e.matmul(ps_y[:, :], w2_sb[:, i_, :], hid[:, i_, :], start=i_ == 0, stop=i_ == C0 - 1)
                        for m in after.get((loop, C0 + i_), ()):
                            unit(m)
                        if i_ == C0 - 1:
                            i.then_inc(w.y_ps, 1)
                    if loop == LOOPS - 1:
                        e.wait_ge(w.cb_ok, E0 * LOOPS)
                        shift_rows()
                        e.wait_ge(w.mpt_ok, 1)
                    e.wait_ge(w.yT_ok, loop + 1)
                    e.wait_ge(w.cb_ok, E0 * (loop + 1))
                    transposed(lambda t: yT[:, t * P:(t + 1) * P], lambda t: ps_m[:, t * P:(t + 1) * P],
                               ident, w.yN_ps)

                def heads(g):
                    return [(0, 2 * g), (0, 2 * g + 1), (1, 2 * g), (1, 2 * g + 1)]

                def scores(v, pair):
                    if v == 0:
                        e.wait_ge(w.max_ok, UNITS)
                        e.wait_ge(w.shift_ok, 32)
                    else:
                        e.wait_ge(w.p_ok, 2 * (v - 1) + pair + 1)
                    for a in range(2):
                        half, j = heads(v // NT)[2 * pair + a]
                        at = slice(64 * half, 64 * half + ROWS + PIECES)
                        kt = v % NT
                        i = e.matmul(ps_s[:, 2 * pair + a, :], k_st[at, j, kt * P:(kt + 1) * P], q_st[at, j, :],
                                     start=True, stop=True)
                    i.then_inc(w.s2_ps, 1)

                def values(v):
                    g, kt = v // NT, v % NT
                    e.wait_ge(w.p_ok, 2 * v + 2)
                    if kt == 0:
                        if g >= 2:
                            e.wait_ge(w.o_ok, g - 1)
                        else:
                            e.wait_ge(w.h_ok, C0 * LOOPS)
                    for a, (half, j) in enumerate(heads(g)):
                        i = e.matmul(ps_u[32 * a:32 * a + 32, g % 2, :], v_aug[:, kt * H + HJ * half + j, :],
                                     probs[:, v % 2, a, :], start=kt == 0, stop=kt == NT - 1,
                                     tile_position=(0, 32 * a))
                    i.then_inc(w.pv_ps, 1)

                def back(g):
                    e.wait_ge(w.o_ok, g + 1)
                    if g:
                        e.wait_ge(w.on_ok, g)
                    else:
                        e.wait_ge(w.z_ok, LOOPS + 1)
                    transposed(lambda t: o_sb[:, t * P:(t + 1) * P], lambda t: ps_m[:, t * P:(t + 1) * P],
                               ident, w.oN_ps)

                scores(0, 0)
                scores(0, 1)
                for v in range(4 * NT):
                    if v + 1 < 4 * NT:
                        scores(v + 1, 0)
                        scores(v + 1, 1)
                    values(v)
                    if v % NT == 1 and v > NT:
                        back(v // NT - 1)
                back(3)
                e.wait_ge(w.on_ok, 4)
                transposed(lambda t: on[:, t, :, :].rearrange("p g k -> p (g k)"),
                           lambda t: ps_m[:, t * P:(t + 1) * P], ident, w.onT_ps)
                e.wait_ge(w.hT_ok, 1)
                for t in range(NT):
                    i = e.matmul(ps_y[:, t * P:(t + 1) * P], hT[:, t * P:(t + 1) * P], wo, start=True, stop=True)
                i.then_inc(w.att_ps, 1)

                e.wait_ge(w.zs_ok, LOOPS + 1)
                transposed(lambda t: yn[:, t, :], lambda t: ps_m[:, t * P:(t + 1) * P], ident, w.zT_ps)
                e.wait_ge(w.xT_ok, LOOPS + 1)
                e.wait_ge(w.o_ok, 4)
                e.matmul(ps_u[:, 1, :], w_q, xT[:, :], start=True, stop=True).then_inc(w.mq_ps, 1)
                e.matmul(ps_u[:, 0, :], w_mag, xT[:, :], start=True, stop=True).then_inc(w.mq_ps, 1)
                for t in range(NT):
                    i = e.matmul(ps_m[:, t * E1:(t + 1) * E1], xT[:, t * P:(t + 1) * P], wr1,
                                 start=True, stop=True)
                i.then_inc(w.lg_ps, 1)
                e.wait_ge(w.hi_ok, LOOPS + 1)
                for i_ in range(E1):
                    if i_ >= 4:
                        e.wait_ge(w.a_ok, i_ - 3)
                    u, cols = ps_s[:, i_ % 4, :], slice(i_ * P, (i_ + 1) * P)
                    e.matmul(u, v1_hi[:, cols], x_hi[:, :], start=True, stop=False)
                    e.matmul(u, v1_lo[:, cols], x_hi[:, :], start=False, stop=False)
                    if i_ == 0:
                        e.wait_ge(w.lo_ok, LOOPS + 1)
                    e.matmul(u, v1_hi[:, cols], x_lo[:, :], start=False, stop=True).then_inc(w.f_ps, 1)
                choice_rows(3)
                choice(3, 0)
                for i_ in range(E1):
                    if i_ + 1 < E1:
                        choice(3, i_ + 1)
                    e.wait_ge(w.hc_ok, C0 * LOOPS + i_ + 1)
                    i = e.matmul(ps_y[:, :], v2_sb[:, i_, :], hid[:, i_, :], start=i_ == 0, stop=i_ == E1 - 1)
                i.then_inc(w.y_ps, 1)
                e.wait_ge(w.yT_ok, LOOPS + 1)
                e.wait_ge(w.cb_ok, E0 * 3)
                transposed(lambda t: yT[:, t * P:(t + 1) * P], lambda t: ps_m[:, t * P:(t + 1) * P],
                           ident, w.yN_ps)
                e.wait_ge(w.ri_ok, 2)
                e.wait_ge(w.sq_ok, CTX)
                for t in range(NT):
                    for k, src in enumerate((ctxt, ctx2)):
                        for c in range(CTX):
                            i = e.matmul(ps_u[:, 0, 2 * t + k:2 * t + k + 1], src[:, c, t * P:(t + 1) * P],
                                         mean_col[:, :], start=c == 0, stop=c == CTX - 1)
                i.then_inc(w.st_ps, 1)
                e.wait_ge(w.a_ok, E1)
                for t in range(NT):
                    for c in range(CTX):
                        i = e.matmul(ps_s[:, t, 0:G1], ctxt[:, c, t * P:(t + 1) * P], w1g[:, c, :],
                                     start=c == 0, stop=c == CTX - 1)
                    i.then_inc(w.g_ps, 1)
                e.wait_ge(w.var_ok, 1)
                for t in range(NT):
                    e.wait_ge(w.ge_ok, t + 1)
                    for c in range(2):
                        i = e.transpose(ps_u[:, c, t * P:(t + 1) * P], ga[:, t, c * P:(c + 1) * P], ident)
                i.then_inc(w.gT_ps, 1)
                e.wait_ge(w.gT_ok, 1)
                e.wait_ge(w.gate_ok, 2)
                for t in range(NT):
                    o = ps_m[:, t * P:(t + 1) * P]
                    for c in range(2):
                        e.matmul(o, gT[:, c, t * P:(t + 1) * P], w2m[:, c, :], start=c == 0, stop=False)
                    i = e.matmul(o, ones[0:1, :], rows_sb[:, G1:G1 + D], start=False, stop=True)
                i.then_inc(w.mlp_ps, 1)
                meet(e, "pe")

        @block.scalar
        def _(e):
            a = e.activation
            e.wait_ge(set_up, 11)
            a(sin_phi[:, :], ws[:, :], ACT.Sin).then_inc(set_act, 1)
            a(cos_phi[:, :], ph_abs, ACT.Sin, bias=half_pi[:, :], scale=-1.0).then_inc(set_act, 1)
            e.wait_ge(set_act, 3)
            e.copy(w1_sums[:, :], ps_s[:, 0, 0:G1]).then_inc(set_pool, 1)
            e.copy(b1_all[:, :], ps_s[:, 1, 0:G1]).then_inc(set_pool, 1)
            e.wait_ge(set_pool, 2)

            def choices(n, at):
                if at < 0:
                    e.wait_ge(w.ct_ps, n)
                    e.copy(ct[:, :], ps_m16[0:PIECES * E0, 0:S]).then_inc(w.ct_ok, 1)
                else:
                    e.wait_ge(w.cb_ps, E0 * (n - 1) + at + 1)
                    e.copy(cb[:, at, :], ps_m[:, :]).then_inc(w.cb_ok, 1)

            with e.Fori(0, B):
                e.wait_ge(w.zT_ps, 1)
                e.copy(hT[:, :], ps_m[:, :]).then_inc(w.xnT_ok, 1)
                for which in range(2):
                    e.wait_ge(w.qkv_ps, which + 1)
                    e.copy(parts[:, which, 0, :], ps_u[:, which, :]).then_inc(w.part_ok, 1)
                for which in range(2):
                    e.wait_ge(w.rest_ok, which + 1)
                    e.copy(parts[:, which, 1, :], rest[:, which, :]).then_inc(w.part_ok, 1)
                for loop in range(LOOPS):
                    e.wait_ge(w.zT_ps, loop + 2)
                    a(xT[:, :], ps_m[:, :], ACT.Copy, scale=f_("norm_w")).then_inc(w.xT_ok, 1)
                    for i in range(C0):
                        if i == 4:
                            e.wait_ge(w.lt_in, loop + 1)
                            a(lt[:, :, :], ld[:, :, :], ACT.Tanh, scale=0.5).then_inc(w.lt_ok, 1)
                        e.wait_ge(w.u_ps, C0 * loop + i + 1)
                        a(hid[:, i, :], ps_u[:, i % 2, :], ACT.Silu).then_inc(w.h_ok, 1)
                    for at in range(-1, E0):
                        choices(loop + 1, at)
                    e.wait_ge(w.y_ps, loop + 1)
                    e.copy(yT[:, :], ps_y[:, :]).then_inc(w.yT_ok, 1)
                for v in range(4 * NT):
                    if v >= 2:
                        e.wait_ge(w.pv_ps, v - 1)
                    for pair in range(2):
                        e.wait_ge(w.s2_ps, 2 * v + pair + 1)
                        a(probs[:, v % 2, 2 * pair:2 * pair + 2, :], ps_s[:, 2 * pair:2 * pair + 2, :], ACT.Exp,
                          scale=float(HD) ** -0.5).then_inc(w.p_ok, 1)
                e.wait_ge(w.z_ok, LOOPS + 1)
                a(gate[:, :], z[:, :, :].rearrange("p t d -> p (t d)"), ACT.Silu).then_inc(w.gate_ok, 1)
                e.wait_ge(w.onT_ps, 1)
                e.copy(hT[:, :], ps_m[:, :]).then_inc(w.hT_ok, 1)
                e.wait_ge(w.zT_ps, LOOPS + 2)
                e.copy(xT[:, :], ps_m[:, :]).then_inc(w.xT_ok, 1)
                e.wait_ge(w.mq_ps, 2)
                a(tg, ps_u[:, 0, :], ACT.Tanh, bias=b_mag_half[:, :], scale=0.5).then_inc(w.tg_ok, 1)

                def relu(i):
                    e.wait_ge(w.f_ps, i + 1)
                    a(hid[:, i, :], ps_s[:, i % 4, :], ACT.Relu).then_inc(w.r_ok, 1)

                for i in range(3):
                    relu(i)
                e.wait_ge(w.ph_ok, 2)
                a(sq, phq, ACT.Sin).then_inc(w.sc_ok, 1)
                a(cq, ph_abs, ACT.Sin, bias=half_pi[:, :], scale=-1.0).then_inc(w.sc_ok, 1)
                e.wait_ge(w.acc_ok, 1)
                a(acc[:, :], acc[:, :], ACT.Sqrt, bias=tiny[:, :], scale=MAG).then_inc(w.inv_in, 1)
                for i in range(3, E1):
                    relu(i)
                for at in range(-1, E0):
                    choices(3, at)
                for c in range(2):
                    e.wait_ge(w.c01_ok, c + 1)
                    a(ctx2[:, c, :], ctxt[:, c, :], ACT.Square).then_inc(w.sq_ok, 1)
                for c in range(2):
                    e.wait_ge(w.ri_ok, c + 1)
                    a(ctx2[:, 2 + c, :], ctxt[:, 2 + c, :], ACT.Square).then_inc(w.sq_ok, 1)
                e.wait_ge(w.y_ps, LOOPS + 1)
                e.copy(yT[:, :], ps_y[:, :]).then_inc(w.yT_ok, 1)
                e.wait_ge(w.yN_ps, LOOPS + 1)
                e.wait_ge(w.x1_ok, 1)
                a(gate[:, :], ps_m[:, :], ACT.Silu).then_inc(w.gate_ok, 1)
                for t in range(NT):
                    e.wait_ge(w.ga_ok, t + 1)
                    a(ga[:, t, :], ga[:, t, :], ACT.Gelu).then_inc(w.ge_ok, 1)
                e.wait_ge(w.gT_ps, 1)
                e.copy(gT[:, :, :], ps_u[:, :, :]).then_inc(w.gT_ok, 1)
                meet(e, "act")

        @block.gpsimd
        def _(e):
            count = [0]

            def link(ins):
                count[0] += 1
                ins.then_inc(w.pool, 1)
                e.wait_ge(w.pool, count[0])

            def power(dst, src, scale, eps, done):
                link(e.tensor_scalar(dst, src, scale, eps, ALU.mult, ALU.add))
                e.tensor_tensor(dst, dst, minus_half[:, :], ALU.pow).then_inc(done, 1)

            e.wait_ge(set_up, 12)
            with e.Fori(0, B):
                count[0] = 0
                e.wait_ge(w.stats0, 1)
                power(rstd[:, :], mv[:, :, 1], 1.0, 1e-5, w.rstd_ok)

                for loop in range(LOOPS):
                    e.wait_ge(w.ssq_ok, loop + 1)
                    e.wait_ge(w.z_ok, loop + 1)
                    power(rstd[:, :], ssq[:, :], 1.0 / D, 1e-6, w.rstd_ok)
                    for i in range(C0):
                        e.wait_ge(w.h_ok, C0 * loop + i + 1)
                        e.wait_ge(w.cb_ok, E0 * loop + i // 2 + 1)
                        e.tensor_tensor(hid[:, i, :], hid[:, i, :], cb[:, i // 2, :], ALU.mult
                                        ).then_inc(w.hc_ok, 1)
                e.wait_ge(w.stats0, 2)
                power(rstd[:, :], mv[:, :, 1], 1.0, 1e-5, w.rstd_ok)
                e.wait_ge(w.sg_in, 1)
                e.tensor_tensor(le[:, :, 0:E1], euler[:, :].rearrange("p (t x) -> p t x", t=NT),
                                ld[:, :, 0:E1], ALU.pow).then_inc(w.sg_ok, 1)
                e.wait_ge(w.xT_ok, LOOPS + 1)
                e.tensor_tensor(ctxt[:, 0, :], xT[:, :], cos_phi[:, :], ALU.mult).then_inc(w.c01_ok, 1)
                e.tensor_tensor(ctxt[:, 1, :], xT[:, :], sin_phi[:, :], ALU.mult).then_inc(w.c01_ok, 1)
                for i in range(2):
                    e.wait_ge(w.a_ok, i + 1)
                    e.wait_ge(w.cb_ok, E0 * LOOPS + i + 1)
                    e.tensor_tensor(hid[:, i, :], hid[:, i, :], cb[:, i, :], ALU.mult).then_inc(w.hc_ok, 1)
                e.wait_ge(w.mem_ok, 1)
                e.wait_ge(w.sc_ok, 2)
                e.tensor_tensor(wc, mem_r, cq, ALU.mult).then_inc(w.rot_in, 1)
                e.tensor_tensor(ws[:, :], mem_r, sq, ALU.mult).then_inc(w.rot_in, 1)
                for i in range(2, E1):
                    e.wait_ge(w.a_ok, i + 1)
                    e.wait_ge(w.cb_ok, E0 * LOOPS + i + 1)
                    e.tensor_tensor(hid[:, i, :], hid[:, i, :], cb[:, i, :], ALU.mult).then_inc(w.hc_ok, 1)
                e.wait_ge(w.var_ok, 1)
                power(rstd[:, :], var[:, :], 1.0, 1e-5, w.rstd_ok)
                meet(e, "pool")

        @block.vector
        def _(e):
            setup = [0]

            def step(ins):
                setup[0] += 1
                ins.then_inc(set_up, 1)
                e.wait_ge(set_up, setup[0])

            tt, ts, stt = e.tensor_tensor, e.tensor_scalar, e.scalar_tensor_tensor

            def reduce_turns(chain, x_, t_):
                chain(ts(t_, x_, float(1 / (2 * np.pi)), ROUND, ALU.mult, ALU.add))
                chain(ts(t_, t_, ROUND, None, ALU.subtract))
                chain(stt(x_, t_, -TWO_PI_A, x_, ALU.mult, ALU.add))
                chain(stt(x_, t_, -TWO_PI_B, x_, ALU.mult, ALU.add))

            for tile, value in ((ones, 1.0), (ones_row, 1.0), (mean_col, 1.0 / (CTX * P)),
                                (half_pi, float(np.pi / 2)), (tiny, 1e-8), (minus_half, -0.5),
                                (euler, float(np.e)), (v_aug, 0.0)):
                if tile is v_aug:
                    i = e.memset(v_aug[:, :, :], 0.0)
                else:
                    i = e.memset(tile[:, :], value)
            e.wait_ge(first_in, 16)
            step(ts(phi[:, :], f_("pos"), f_("phases"), 0.01, ALU.mult, ALU.mult))
            step(e.tensor_copy(ws[:, :], phi[:, :]))
            reduce_turns(step, ws[:, :], wc)
            step(stt(ph_abs, ws[:, :], -1.0, ws[:, :], ALU.mult, ALU.max))
            step(ts(ws[:, :], ws[:, :], PI_BELOW, -PI_BELOW, ALU.min, ALU.max))
            step(e.memset(v_aug[:, :, HD:HD + 1], 1.0))
            step(e.memset(k_st[32:64, :, :], 1.0))
            step(e.memset(k_st[96:128, :, :], 1.0))
            step(e.tensor_copy(ident_b[:, :], ident))
            e.wait_ge(w_in, 48)
            e.tensor_copy(select_sb[:, :], hid[0:PIECES * E0, 6:8, :].rearrange("p a n -> p (a n)"))
            wv1 = hid[:, 0:4, :].rearrange("p a n -> p (a n)")
            vv1 = hid[:, 4:6, :].rearrange("p a n -> p (a n)")
            e.tensor_copy(w1_hi[:, :], wv1)
            step(e.tensor_copy(v1_hi[:, :], vv1))
            tt(w1_lo[:, :], wv1, w1_hi[:, :].bitcast(F32), ALU.subtract)
            step(tt(v1_lo[:, :], vv1, v1_hi[:, :].bitcast(F32), ALU.subtract))
            e.wait_ge(second_in, 32)
            for c in range(CTX):
                ts(w1g[:, c, :], w1m[:, c, :], f_("ln_g")[:, c:c + 1], None, ALU.mult)
                ts(hid[:, 8, c * P:(c + 1) * P], ones[:, :], f_("ln_b")[:, c:c + 1], None, ALU.mult)
            e.tensor_scalar(b_mag_half[:, :], f_("b_mag"), 0.5, None, ALU.mult).then_inc(set_pe, 1)
            e.wait_ge(set_pe, 1)
            e.wait_ge(set_pool, 2)
            e.wait_ge(v_in, 32)

            count = [0]

            def link(ins):
                count[0] += 1
                ins.then_inc(w.dve, 1)
                e.wait_ge(w.dve, count[0])

            def layernorm(src, dst, n_rstd, done):
                for t in range(NT):
                    i = e.bn_stats(bn6[:, t, :], src[:, t, :])
                link(i)
                for t in range(NT):
                    i = e.bn_aggr(mv[:, t, :], bn6[:, t, :])
                i.then_inc(w.stats0, 1)
                e.wait_ge(w.rstd_ok, n_rstd)
                for t in range(NT):
                    i = ts(dst[:, t, :], src[:, t, :], mv[:, t, 0:1], rstd[:, t:t + 1], ALU.subtract, ALU.mult)
                i.then_inc(done, 1)

            def split_x(n):
                e.wait_ge(w.xT_ok, n)
                e.tensor_copy(x_hi[:, :], xT[:, :]).then_inc(w.hi_ok, 1)
                e.wait_ge(w.hi_ok, n)
                tt(x_lo[:, :], xT[:, :], x_hi[:, :].bitcast(F32), ALU.subtract).then_inc(w.lo_ok, 1)

            def rank_of(p, n, mask):
                sh = [P, NT, n, n]
                mine = p.unsqueeze(3).to_broadcast(sh)
                theirs = p.unsqueeze(2).to_broadcast(sh)
                b4 = beat[:, 0:NT * n * n].rearrange("p (t i j) -> p t i j", t=NT, i=n)
                t4 = tie[:, 0:NT * n * n].rearrange("p (t i j) -> p t i j", t=NT, i=n)
                tt(b4, theirs, mine, ALU.is_gt)
                link(tt(t4, theirs, mine, ALU.is_equal))
                link(tt(t4, t4, mask, ALU.mult))
                link(tt(b4, b4, t4, ALU.add))
                rk = rank[:, 0:NT * n].rearrange("p (t i) -> p t i", t=NT)
                link(e.tensor_reduce(rk, b4, AX.X, ALU.add))
                return rk

            def bcast(v, n):
                return v.unsqueeze(2).to_broadcast([P, NT, n])

            def split_choice():
                link(e.tensor_copy(cp[:, :, 0:E0], cw[:, :, :]))
                link(tt(crest[:, :, :], cw[:, :, :], cp[:, :, 0:E0], ALU.subtract))
                link(e.tensor_copy(cp[:, :, E0:2 * E0], crest[:, :, :]))
                tt(cp[:, :, 2 * E0:3 * E0], crest[:, :, :], cp[:, :, E0:2 * E0], ALU.subtract
                   ).then_inc(w.cp_ok, 1)

            low4 = lower[:, 0:16].rearrange("p (i j) -> p i j", i=4)
            low8 = lower[:, 64:128].rearrange("p (i j) -> p i j", i=8)

            def router0_a(loop):
                e.wait_ge(w.lg_ps, loop + 1)
                link(e.tensor_copy(lg[:, :, :], ps_m[:, 0:NT * 12].rearrange("p (t x) -> p t x", t=NT)))
                pair = lg[:, :, 4:12].rearrange("p t (g e) -> p t g e", e=2)
                e.tensor_reduce(lm[:, :, 0:1], lg[:, :, 0:4], AX.X, ALU.max)
                link(e.tensor_reduce(lm[:, :, 1:5], pair, AX.X, ALU.max))
                tt(ld[:, :, 0:4], lg[:, :, 0:4], lm[:, :, 0:1].to_broadcast([P, NT, 4]), ALU.subtract)
                tt(ld[:, :, 4:12].rearrange("p t (g e) -> p t g e", e=2), pair,
                   lm[:, :, 1:5].unsqueeze(3).to_broadcast([P, NT, 4, 2]), ALU.subtract).then_inc(w.lt_in, 1)

            def router0_b(loop):
                e.wait_ge(w.lt_ok, loop + 1)
                link(ts(ld[:, :, :], lt[:, :, :], -1.0, 1.0, ALU.mult, ALU.add))
                link(e.reciprocal(ld[:, :, :], ld[:, :, :]))
                link(stt(le[:, :, :].rearrange("p t x -> p (t x)"), lt[:, :, :].rearrange("p t x -> p (t x)"), 1.0,
                         ld[:, :, :].rearrange("p t x -> p (t x)"), ALU.add, ALU.mult))
                pair = le[:, :, 4:12].rearrange("p t (g e) -> p t g e", e=2)
                e.tensor_reduce(lm[:, :, 0:1], le[:, :, 0:4], AX.X, ALU.add)
                link(e.tensor_reduce(lm[:, :, 1:5], pair, AX.X, ALU.add))
                link(e.reciprocal(lm[:, :, :], lm[:, :, :]))
                tt(le[:, :, 0:4], le[:, :, 0:4], lm[:, :, 0:1].to_broadcast([P, NT, 4]), ALU.mult)
                link(tt(pair, pair, lm[:, :, 1:5].unsqueeze(3).to_broadcast([P, NT, 4, 2]), ALU.mult))
                rk = rank_of(lg[:, :, 0:4], 4, low4.unsqueeze(1).to_broadcast([P, NT, 4, 4]))
                link(stt(gw[:, :, :], rk, 1.5, le[:, :, 0:4], ALU.is_lt, ALU.mult))
                link(e.tensor_reduce(wsum[:, :], gw[:, :, :], AX.X, ALU.add))
                link(ts(wsum[:, :], wsum[:, :], 1e-9, None, ALU.add))
                link(e.reciprocal(wsum[:, :], wsum[:, :]))
                tt(gw[:, :, :], gw[:, :, :], bcast(wsum[:, :], 4), ALU.mult)
                link(e.tensor_reduce(lm[:, :, 1:5], pair, AX.X, ALU.max))
                link(ts(ld[:, :, 0:4], lm[:, :, 1:5], 1e-9, None, ALU.add))
                link(e.reciprocal(ld[:, :, 0:4], ld[:, :, 0:4]))
                link(tt(lm[:, :, 1:5], lm[:, :, 1:5], ld[:, :, 0:4], ALU.mult))
                tt(gw[:, :, :], gw[:, :, :], lm[:, :, 1:5], ALU.mult)
                link(tt(ld[:, :, 4:8], pair[:, :, :, 0], pair[:, :, :, 1], ALU.is_ge))
                cwp = cw[:, :, :].rearrange("p t (g e) -> p t g e", e=2)
                link(tt(cwp[:, :, :, 0], ld[:, :, 4:8], gw[:, :, :], ALU.mult))
                link(tt(cwp[:, :, :, 1], gw[:, :, :], cwp[:, :, :, 0], ALU.subtract))
                split_choice()

            def max_of(n):
                e.wait_ge(w.s1_ps, n + 1)
                t = 2 * (n % 2)
                e.tensor_reduce(smax[:, t:t + 2, n // 2], ps_s[:, t:t + 2, :], AX.X, ALU.max).then_inc(w.max_ok, 1)

            with e.Fori(0, B):
                count[0] = 0
                e.wait_ge(x_in, 16)
                e.nop().then_inc(x_in, -16)
                layernorm(xin, z, 1, w.z_ok)
                e.wait_ge(w.z_ok, 1)

                def rms(loop):
                    for t in range(NT):
                        i = e.tensor_tensor_reduce(zs[:, t, :], z[:, t, :], z[:, t, :], 1.0, 0.0, ALU.mult,
                                                   ALU.add, ssq[:, t:t + 1])
                    i.then_inc(w.ssq_ok, 1)
                    e.wait_ge(w.rstd_ok, loop + 2)
                    for t in range(NT):
                        i = ts(zs[:, t, :], z[:, t, :], rstd[:, t:t + 1], None, ALU.mult)
                    i.then_inc(w.zs_ok, 1)

                for which in range(2):
                    e.wait_ge(w.part_ok, which + 1)
                    tt(rest[:, which, :], ps_u[:, which, :], parts[:, which, 0, :], ALU.subtract
                       ).then_inc(w.rest_ok, 1)
                rms(0)
                for which in range(2):
                    e.wait_ge(w.part_ok, which + 3)
                    tt(parts[:, which, 2, :], rest[:, which, :], parts[:, which, 1, :], ALU.subtract
                       ).then_inc(w.parts_ok, 1)
                e.wait_ge(w.qkv_ps, 3)
                e.tensor_copy(v_aug[:, :, 0:HD], ps_y[:, :].rearrange("p (a v) -> p a v", v=HD)
                              ).then_inc(w.v_ok, 1)
                for loop in range(LOOPS):
                    split_x(loop + 1)
                    router0_a(loop)
                    router0_b(loop)
                    for (lp, _), ns in sorted(after.items()):
                        if lp == loop:
                            for n in ns:
                                max_of(n)
                    if loop == LOOPS - 1:
                        e.wait_ge(w.max_ok, UNITS)
                        link(ts(mp[:, :, 0:H], smax[:, :, :], -1.0, None, ALU.mult))
                        link(stt(mrest[:, :, :], smax[:, :, :], -1.0, mp[:, :, 0:H], ALU.mult, ALU.subtract))
                        link(e.tensor_copy(mp[:, :, H:2 * H], mrest[:, :, :]))
                        tt(mp[:, :, 2 * H:3 * H], mrest[:, :, :], mp[:, :, H:2 * H], ALU.subtract
                           ).then_inc(w.mp_ok, 1)
                        e.wait_ge(w.mpt_ps, 1)
                        e.tensor_copy(mpt[:, :], ps_m16[0:PIECES * H, 0:S]).then_inc(w.mpt_ok, 1)
                    e.wait_ge(w.yN_ps, loop + 1)
                    zf = z[:, :, :].rearrange("p t d -> p (t d)")
                    tt(zf, zf, ps_m[:, :], ALU.add).then_inc(w.z_ok, 1)
                    e.wait_ge(w.z_ok, loop + 2)
                    if loop + 1 < LOOPS:
                        rms(loop + 1)
                for g in range(4):
                    e.wait_ge(w.pv_ps, NT * (g + 1))
                    if g:
                        e.wait_ge(w.oN_ps, g)
                    e.tensor_copy(o_sb[:, :], ps_u[:, g % 2, :]).then_inc(w.o_ok, 1)
                    e.wait_ge(w.oN_ps, g + 1)
                    src = ps_m[:, :].rearrange("p (a k) -> p a k", k=32)
                    link(e.reciprocal(oden[:, :, :], src[:, :, HD:HD + 1]))
                    dst = on[:, :, g, :].rearrange("p t (a v) -> p t a v", v=HD)
                    tt(dst, ps_m[:, :].rearrange("p (t a k) -> p t a k", t=NT, k=32)[:, :, :, 0:HD],
                       oden[:, :, 0].rearrange("p (t a) -> p t a", t=NT).unsqueeze(3).to_broadcast([P, NT, 4, HD]),
                       ALU.mult).then_inc(w.on_ok, 1)
                x1f, xf = (v[:, :, :].rearrange("p t d -> p (t d)") for v in (x1, xin))
                ynf, of = (v[:, :, :].rearrange("p t d -> p (t d)") for v in (yn, outb))
                e.wait_ge(w.att_ps, 1)
                e.wait_ge(w.gate_ok, 1)
                link(tt(x1f, ps_y[:, :], gate[:, :], ALU.mult))
                tt(x1f, x1f, xf, ALU.add).then_inc(w.x1_ok, 1)
                e.wait_ge(w.x1_ok, 1)
                layernorm(x1, yn, LOOPS + 2, w.zs_ok)

                split_x(LOOPS + 1)
                e.wait_ge(w.mq_ps, 1)
                link(stt(phq, ps_u[:, 1, :], f_("b_q"), phi[:, :], ALU.add, ALU.add))
                e.wait_ge(w.lg_ps, LOOPS + 1)
                ts(ld[:, :, 0:E1], ps_m[:, 0:NT * E1].rearrange("p (t x) -> p t x", t=NT), -1.0, None, ALU.mult
                   ).then_inc(w.sg_in, 1)
                reduce_turns(link, phq, turns)
                stt(ph_abs, phq, -1.0, phq, ALU.mult, ALU.max).then_inc(w.ph_ok, 1)
                e.wait_ge(w.ph_ok, 1)
                ts(phq, phq, PI_BELOW, -PI_BELOW, ALU.min, ALU.max).then_inc(w.ph_ok, 1)
                e.wait_ge(w.tg_ok, 1)
                e.tensor_tensor_scan(acc[:, :], tg, ones_row[:, :], 0.0, ALU.add, ALU.add
                                     ).then_inc(w.acc_ok, 1)
                link(stt(wgt, tg, 1.0, xT[:, :], ALU.add, ALU.mult))
                tt(wc, wgt, cos_phi[:, :], ALU.mult)
                link(tt(ws[:, :], wgt, sin_phi[:, :], ALU.mult))
                e.tensor_tensor_scan(mem_r, ones_row[:, :], wc, 0.0, ALU.mult, ALU.add)
                link(e.tensor_tensor_scan(mem_i, ones_row[:, :], ws[:, :], 0.0, ALU.mult, ALU.add))

                def squared(i):
                    e.wait_ge(w.r_ok, i + 1)
                    stt(hid[:, i, :], ps_s[:, i % 4, :], 0.0, hid[:, i, :], ALU.max, ALU.mult).then_inc(w.a_ok, 1)

                for i in range(3):
                    squared(i)
                e.wait_ge(w.sg_ok, 1)
                link(ts(le[:, :, 0:E1], le[:, :, 0:E1], 1.0, None, ALU.add))
                link(e.reciprocal(lg[:, :, 0:E1], le[:, :, 0:E1]))
                rk = rank_of(lg[:, :, 0:E1], E1, low8.unsqueeze(1).to_broadcast([P, NT, E1, E1]))
                link(stt(cw[:, :, :], rk, 1.5, lg[:, :, 0:E1], ALU.is_lt, ALU.mult))
                link(e.tensor_reduce(wsum[:, :], cw[:, :, :], AX.X, ALU.add))
                link(ts(wsum[:, :], wsum[:, :], 1e-20, None, ALU.add))
                link(e.reciprocal(wsum[:, :], wsum[:, :]))
                link(tt(cw[:, :, :], cw[:, :, :], bcast(wsum[:, :], E1), ALU.mult))
                split_choice()
                e.wait_ge(w.inv_in, 1)
                link(e.reciprocal(inv[:, :], acc[:, :]))
                stt(mem_r, mem_r, MAG, inv[:, :], ALU.mult, ALU.mult).then_inc(w.mem_ok, 1)
                link(stt(mem_i, mem_i, MAG, inv[:, :], ALU.mult, ALU.mult))
                for i in range(3, E1):
                    squared(i)
                e.wait_ge(w.sc_ok, 2)
                tt(turns, mem_i, sq, ALU.mult)
                link(tt(mem_i, mem_i, cq, ALU.mult))
                e.wait_ge(w.rot_in, 2)
                tt(ctxt[:, 2, :], wc, turns, ALU.add).then_inc(w.ri_ok, 1)
                tt(ctxt[:, 3, :], mem_i, ws[:, :], ALU.subtract).then_inc(w.ri_ok, 1)
                e.wait_ge(w.st_ps, 1)
                link(e.tensor_copy(stat[:, :, :], ps_u[:, 0, 0:2 * NT].rearrange("p (t k) -> p t k", k=2)))
                link(tt(var[:, :], stat[:, :, 0], stat[:, :, 0], ALU.mult))
                tt(var[:, :], stat[:, :, 1], var[:, :], ALU.subtract).then_inc(w.var_ok, 1)
                e.wait_ge(w.rstd_ok, LOOPS + 3)
                link(stt(nmr[:, :], stat[:, :, 0], -1.0, rstd[:, :], ALU.mult, ALU.mult))
                for t in range(NT):
                    i = stt(gb[:, t, :], w1_sums[:, :], nmr[:, t:t + 1], b1_all[:, :], ALU.mult, ALU.add)
                link(i)
                for t in range(NT):
                    e.wait_ge(w.g_ps, t + 1)
                    stt(ga[:, t, :], ps_s[:, t, 0:G1], rstd[:, t:t + 1], gb[:, t, :], ALU.mult, ALU.add
                        ).then_inc(w.ga_ok, 1)
                e.wait_ge(w.mlp_ps, 1)
                link(tt(of, ps_m[:, :], ynf, ALU.add))
                link(tt(of, of, gate[:, :], ALU.mult))
                tt(of, of, x1f, ALU.add).then_inc(w.out_ok, 1)
                meet(e, "dve")


_INPUTS = ("x", "first", "second", "w1", "w2", "v1", "v2", "rows", "select")


def _layouts(i):
    a = {k: np.asarray(v) for k, v in i.items()}
    by_half = lambda v: v.reshape(2, HJ, D, HD).transpose(2, 0, 3, 1).reshape(D, D)
    column = lambda v: v.reshape(-1, P).T
    first = dict(
        ident=np.eye(P, dtype=np.float32),
        wq=by_half(a["L0_attn_W_query"]),
        wk=by_half(a["L0_attn_W_key"]),
        wv=a["L0_attn_W_val"].transpose(1, 0, 2).reshape(D, D),
        wr=np.concatenate([a["L0_ffn_w_macro"], a["L0_ffn_w_micro"].reshape(E0, D)]).T,
        norm_w=column(a["L0_ffn_norm_w"]),
        phases=column(a["L1_attn_random_phases"]),
        b_mag=column(a["L1_attn_b_mag"]),
        b_q=column(a["L1_attn_b_q"]),
        ln_g=column(a["L1_attn_ln_g"]),
        ln_b=column(a["L1_attn_ln_b"]),
        pos=np.broadcast_to(np.arange(S, dtype=np.float32), (P, S)),
    )
    return a, first, column


def kernel(**inputs):
    import concourse.bacc as bacc
    from concourse.bass_utils import run_bass_kernel_spmd as run

    a, first, column = _layouts(inputs)
    low = np.zeros((P, 2, 64), np.float32)
    low[:, 0, :16] = np.tril(np.ones((4, 4), np.float32), -1).ravel()
    low[:, 1, :] = np.tril(np.ones((8, 8), np.float32), -1).ravel()
    first["lower"] = low.reshape(P, 128)
    second = dict(
        wo=a["L0_attn_W_out"].reshape(2, 4, 2, HD, D).transpose(1, 0, 2, 3, 4).reshape(D, D),
        w_mag=a["L1_attn_W_mag"].T,
        w_q=a["L1_attn_W_q"].T,
        w2m=a["L1_attn_W2"].reshape(D, 2, P).transpose(2, 1, 0).reshape(P, G1),
        wr1=a["L1_ffn_router_w"].T,
        w1m=a["L1_attn_W1"].reshape(G1, CTX, P).transpose(2, 1, 0).reshape(P, CTX * G1),
    )
    select = np.zeros((PIECES, E0, E0, P), np.float32)
    for ex in range(E0):
        select[:, ex, ex, :] = 1.0
    arrays = dict(
        x=a["L0_attn_q"],
        first=np.concatenate([first[n] for n in FIRST], axis=1),
        second=np.concatenate([second[n] for n in SECOND], axis=1),
        w1=a["L0_ffn_w1"].reshape(E0 * F0, D).T,
        w2=a["L0_ffn_w2"].reshape(E0, D, 2, P).transpose(3, 0, 2, 1).reshape(P, C0 * D),
        v1=a["L1_ffn_w1"],
        v2=a["L1_ffn_w2"].reshape(E1, P, D).transpose(1, 0, 2).reshape(P, E1 * D),
        rows=np.concatenate([a["L1_attn_b1"], a["L1_attn_b2"]])[None, :],
        select=select.reshape(PIECES * E0, E0 * P),
    )
    nc = bacc.Bacc("TRN2", target_bir_lowering=False, num_devices=1)
    args, sent = [], {}
    for name in _INPUTS:
        v = np.ascontiguousarray(arrays[name])
        sent[f"in_{name}"] = v
        args.append(nc.dram_tensor(f"in_{name}", v.shape, mybir.dt.from_np(v.dtype), kind="ExternalInput").ap())
    args.append(nc.dram_tensor("out_0", (B, S, D), F32, kind="ExternalOutput").ap())
    build(nc, *args)
    return run(nc, [sent], core_ids=[0]).results[0]["out_0"]
```

```python
from contextlib import ExitStack

import numpy as np

import concourse.bass as bass
from concourse import mybir

F32 = mybir.dt.float32
F32R = mybir.dt.float32r
BF16 = mybir.dt.bfloat16
ALU = mybir.AluOpType
ACT = mybir.ActivationFunctionType
AX = mybir.AxisListType

P = 128
B, S, D = 8, 512, 128
NT = S // P
H, HD = 16, 8
HJ = H // 2
PIECES = 3
Q_PART = (0, 0, 0, 1, 1, 2)
K_PART = (0, 1, 2, 0, 1, 0)
ROWS = len(Q_PART) * HD
STACK_Q = ((0, 0, 0, 3), (3 * HD, 1, 0, 2), (5 * HD, 2, 0, 1))
STACK_K = ((0, 0, 1, 3), (3 * HD, 0, 1, 2), (5 * HD, 0, 0, 1))
STACK_DMAS = 2 * (len(STACK_Q) + len(STACK_K)) + 2
E0, F0 = 8, 256
C0 = E0 * F0 // P
LOOPS = 2
GROUPS = 4
E1 = 8
G1 = 2 * D
CTX = 4
ROUND = float(1.5 * 2 ** 23)
TWO_PI_A = 6.28125
TWO_PI_B = float(2 * np.pi - 6.28125)
PI_BELOW = 3.1415925
MAG = 2.5

FIRST = dict(ident=128, wq=128, wk=128, wv=128, wr=GROUPS + E0, norm_w=1, phases=1, b_mag=1, b_q=1,
             ln_g=CTX, ln_b=CTX, lower=128, pos=S)
SECOND = dict(wo=128, w_mag=128, w_q=128, w2m=G1, wr1=E1, w1m=CTX * G1)


def columns(widths, name):
    at = 0
    for n, w in widths.items():
        if n == name:
            return slice(at, at + w)
        at += w


def build(nc, x, first, second, w1, w2, v1, v2, rows, out):
    ctx = ExitStack()
    with ctx:
        def sb(name, shape, dt=F32):
            return ctx.enter_context(nc.sbuf_tensor(name, shape, dt))

        def psum(name, shape, dt=F32):
            return ctx.enter_context(nc.psum_tensor(name, shape, dt))

        c_first = sb("c_first", [P, sum(FIRST.values())])
        c_second = sb("c_second", [P, sum(SECOND.values())])

        def f_(name):
            return c_first[:, columns(FIRST, name)]

        def g_(name):
            return c_second[:, columns(SECOND, name)]

        ident, wq, wk, wv, wr = f_("ident"), f_("wq"), f_("wk"), f_("wv"), f_("wr")
        lower = f_("lower")
        wo, w_mag, w_q, wr1 = g_("wo"), g_("w_mag"), g_("w_q"), g_("wr1")
        w2m = g_("w2m").rearrange("p (c d) -> p c d", c=2)
        w1m = g_("w1m").rearrange("p (c g) -> p c g", c=CTX)
        w1_hi, w1_lo = sb("w1_hi", [P, C0 * P], F32R), sb("w1_lo", [P, C0 * P], F32R)
        v1_hi, v1_lo = sb("v1_hi", [P, E1 * P], F32R), sb("v1_lo", [P, E1 * P], F32R)
        w2_sb, v2_sb = sb("w2_sb", [P, C0, D]), sb("v2_sb", [P, E1, D])
        rows_sb = sb("rows_sb", [1, G1 + D])
        ident_b = sb("ident_b", [P, P], BF16)
        ones = sb("ones", [P, P])
        ones_row = sb("ones_row", [P, S])
        mean_col = sb("mean_col", [P, 1])
        half_pi = sb("half_pi", [P, 1])
        tiny = sb("tiny", [P, 1])
        b_mag_half = sb("b_mag_half", [P, 1])
        minus_half = sb("minus_half", [P, NT])
        euler = sb("euler", [P, NT * E1])
        phi, cos_phi, sin_phi = sb("phi", [P, S]), sb("cos_phi", [P, S]), sb("sin_phi", [P, S])
        w1g = sb("w1g", [P, CTX, G1 + 1])
        b1_all, b2_all = sb("b1_all", [P, G1]), sb("b2_all", [P, D])

        x_next, xin = sb("x_next", [P, NT, D]), sb("xin", [P, NT, D])
        z = sb("z", [P, NT, D])
        zs = sb("zs", [P, NT, D])
        bn6, mv, rstd = sb("bn6", [P, NT, 6]), sb("mv", [P, NT, 2]), sb("rstd", [P, NT])
        bn6_n, mv_n, rstd_n = sb("bn6_n", [P, NT, 6]), sb("mv_n", [P, NT, 2]), sb("rstd_n", [P, NT])
        ssq = sb("ssq", [P, NT])
        xT = sb("xT", [P, S])
        nT = sb("nT", [P, S])
        x_hi, x_lo = sb("x_hi", [P, S], F32R), sb("x_lo", [P, S], F32R)
        parts = sb("parts", [P, 2, PIECES, S], BF16)
        rest = sb("rest", [P, 2, S])
        q_st, k_st = sb("q_st", [P, 2, HJ, S], BF16), sb("k_st", [P, HJ, S], BF16)
        v_aug = sb("v_aug", [P, NT * H, 32])
        hid = sb("hid", [P, C0, S])
        part_y = sb("part_y", [P, 2, NT, D])
        smax = sb("smax", [P, NT, H])
        mrest = sb("mrest", [P, NT, HJ])
        mp = sb("mp", [P, NT, PIECES * HJ], BF16)
        mpt = sb("mpt", [PIECES * HJ, S], BF16)
        probs = sb("probs", [P, 2, 4, S])
        o_sb = sb("o_sb", [P, S])
        oden = sb("oden", [P, NT * 4, 1])
        on = sb("on", [P, NT, 4, 32])
        hT = sb("hT", [P, S])
        gate = sb("gate", [P, NT, D])
        x1 = sb("x1", [P, NT, D])
        outb = sb("outb", [P, NT, D])
        lg = sb("lg", [P, NT, 12])
        lm = sb("lm", [P, NT, 5])
        le = sb("le", [P, NT, 12])
        ld = sb("ld", [P, NT, 12])
        lt = sb("lt", [P, NT, 12])
        beat, tie = sb("beat", [P, NT * 8 * 8]), sb("tie", [P, NT * 8 * 8])
        rank = sb("rank", [P, NT * 8])
        cw = sb("cw", [P, NT, E0])
        wsum = sb("wsum", [P, NT])
        gw = sb("gw", [P, NT, GROUPS])
        tg, wgt, turns, phq = (probs[:, 0, n, :] for n in range(4))
        ph_abs, cq, sq, wc = (probs[:, 1, n, :] for n in range(4))
        ga = probs[:, 0, 0:2, :].rearrange("p a (t g) -> p (a t) g", t=2)
        gT = probs[:, 0, 2:4, :]
        mem = sb("mem", [P, 2, S])
        mem_r, mem_i = mem[:, 0, :], mem[:, 1, :]
        ctxt, squares = hid[:, 8:12, :], hid[:, 12:15, :]
        ws, acc, inv = sb("ws", [P, S]), sb("acc", [P, S]), sb("inv", [P, S])
        stat = sb("stat", [P, NT, 2])
        var = sb("var", [P, NT])
        yn = sb("yn", [P, NT, D])

        scr = [nc.dram_tensor(f"scr_{n}", [PIECES, 2, HD * HJ, S], BF16).ap() for n in "qk"]
        scr_m = nc.dram_tensor("scr_m", [2, PIECES * HJ, S], BF16).ap()
        zeros = nc.dram_tensor("zeros", [PIECES, HJ, S], BF16).ap()

        ps_s = psum("ps_s", [P, 4, S])
        ps_u = psum("ps_u", [P, 2, S])
        ps_y = psum("ps_y", [P, S])
        ps_m = psum("ps_m", [P, S])
        ps_u16 = ps_u[:, 0, :].bitcast(BF16)
        y_bank = (ps_y, ps_m)

        def sem(name):
            return ctx.enter_context(nc.semaphore(name))

        first_in, second_in, v_in = sem("first_in"), sem("second_in"), sem("v_in")
        w_in = sem("w_in")
        x_in, stored, zeroed = sem("x_in"), sem("stored"), sem("zeroed")
        set_up = sem("set_up")
        set_pool, set_pe, set_act = sem("set_pool"), sem("set_pe"), sem("set_act")
        met = sem("met")
        go = {n: sem(f"go_{n}") for n in ("pe", "act", "dve", "pool")}

        body = {}

        for name in (
            "nstats_ok nrstd_ok nz_ok nssq_ok nzs_ok nzT_ps nT_ok qkv_ps part_ok rest_ok parts_ok v_ok "
            "scr_out stack_in x_used ssq_ok rstd_ok zs_ok z_ok zT_ps xT_ok hi_ok lo_ok lg_ps lg_ok lt_in lt_ok "
            "cw_ok u_ps h_ok y_ps yc_ok za_ok s1_ps max_ok mp_ok mpt_ps mpt_ok m_out shift_ok s2_ps p_ok "
            "pv_ps o_ok oN_ps on_ok onT_ps hT_ok att_ps gate_ok x1_ok stats_ok yn_ok ynb_ok mq_ps r_ok tg_ok ph_ok "
            "sc_ok acc_ok inv_in mem_ok f_ps a_ok sg_in sg_ok c01_ok rot_in ri_ok sq_ok g_ps var_ok ga_ok "
            "ge_ok gT_ps gT_ok mlp_ps out_ok dve pool"
        ).split():
            body[name] = sem(name)
        numbers = sorted(int(s.num) for s in body.values())
        assert numbers[-1] - numbers[0] == len(numbers) - 1
        w = type("W", (), body)

        UNITS = 2 * H
        ROUND_UNITS = UNITS // 2
        ORDER = [half * HJ + 2 * g + a for g in range(4) for half in range(2) for a in range(2)]
        after = {}
        for n in range(UNITS):
            if n < ROUND_UNITS:
                at = (0, 15 + n)
            else:
                at = (1, 10 + (n - ROUND_UNITS) * 21 // 16)
            after.setdefault(at, []).append(n)

        block = ctx.enter_context(nc.Block())

        @block.sync
        def _(e):
            def stack(in_body):
                for which in range(2):
                    e.wait_ge(w.parts_ok, which + 1)
                    e.dma_start(scr[which].rearrange("a h r n -> (h r) a n"), parts[:, which, :, :]
                                ).then_inc(w.scr_out, 16)
                if in_body:
                    e.wait_ge(w.s2_ps, 2 * 4 * NT)
                e.wait_ge(w.scr_out, 32)
                for which in range(2):
                    for half in range(2):
                        dst = k_st if which else q_st[:, half]
                        for pattern in (STACK_K if which else STACK_Q):
                            row, first_part, step, n = pattern
                            src = scr[which][first_part:first_part + 1 + step * (n - 1), half]
                            src = src.rearrange("c (k j) n -> k c (j n)", j=HJ)
                            if n > 1 and step == 0:
                                src = src.to_broadcast([HD, n, HJ * S])
                            at = 64 * half + row
                            e.dma_start(dst[at:at + HD * n, :, :].rearrange("r j n -> r (j n)"), src
                                        ).then_inc(w.stack_in, 16)
                for half in range(2):
                    e.dma_start(q_st[64 * half + ROWS:64 * half + ROWS + PIECES, half], zeros
                                ).then_inc(w.stack_in, 16)

            def shift(r):
                e.wait_ge(w.mpt_ok, r + 1)
                e.dma_start(scr_m[r], mpt[:, :]).then_inc(w.m_out, 16)
                e.wait_ge(w.m_out, 16 * (r + 1))
                src = scr_m[r].rearrange("(p g h a) n -> p g h a n", g=2, h=2, a=2)
                for half in range(2):
                    at = 64 * half + ROWS
                    for g in range(2):
                        e.dma_start(q_st[at:at + PIECES, half, 4 * r + 2 * g:4 * r + 2 * g + 2, :], src[:, g, half]
                                    ).then_inc(w.shift_ok, 16)

            def gather():
                e.wait_ge(met, 4)
                e.nop().then_inc(met, -4)
                e.sem_clear(range(numbers[0], numbers[-1] + 1))
                for n in go:
                    e.sem_inc(go[n], 1)

            e.dma_start(x_next[:, :, :], x[0:1].rearrange("o (t p) d -> p (o t) d", p=P)).then_inc(x_in, 16)
            e.dma_start(c_first[:, :], first).then_inc(first_in, 16)
            e.dma_start(hid[:, 0:4, :], w1.rearrange("p (a n) -> p a n", a=4)).then_inc(w_in, 16)
            e.dma_start(c_second[:, :], second).then_inc(second_in, 16)
            e.dma_start(rows_sb[:, :], rows).then_inc(second_in, 16)
            e.dma_start(hid[:, 4:6, :], v1.rearrange("p (a n) -> p a n", a=2)).then_inc(w_in, 16)
            e.wait_ge(set_pool, 1)
            e.dma_start(zeros, q_st[64:64 + PIECES, 0]).then_inc(zeroed, 16)
            e.wait_ge(zeroed, 16)
            stack(False)
            e.dma_start(w2_sb[:, :, :], w2.rearrange("p (c d) -> p c d", c=C0)).then_inc(v_in, 16)
            e.dma_start(v2_sb[:, :, :], v2.rearrange("p (c d) -> p c d", c=E1)).then_inc(v_in, 16)
            e.wait_ge(w.stack_in, 16 * STACK_DMAS)
            e.sem_inc(stored, 16)
            gather()
            with e.Fori(0, B) as b:
                e.wait_ge(w.x_used, 1)
                e.dma_start(x_next[:, :, :], x[bass.ds((b + 1) & (B - 1), 1)].rearrange("o (t p) d -> p (o t) d", p=P)
                            ).then_inc(x_in, 16)
                shift(0)
                shift(1)
                stack(True)
                e.wait_ge(w.out_ok, 1)
                e.dma_start(out[bass.ds(b, 1)].rearrange("o (t p) d -> p (o t) d", p=P), outb[:, :, :]
                            ).then_inc(stored, 16)
                e.wait_ge(w.stack_in, 16 * STACK_DMAS)
                gather()
            e.wait_ge(stored, 16)

        def meet(e, name):
            e.drain().then_inc(met, 1)
            e.wait_ge(go[name], 1)
            e.nop().then_inc(go[name], -1)

        @block.tensor
        def _(e):
            def transposed(src, dst, idt, done):
                for t in range(NT):
                    i = e.transpose(dst(t), src(t), idt)
                i.then_inc(done, 1)

            def next_T(in_body):
                e.wait_ge(w.nz_ok, 1)
                if in_body:
                    e.wait_ge(w.p_ok, 2 * 4 * NT)
                transposed(lambda t: z[:, t, :], lambda t: ps_s[:, 3, t * P:(t + 1) * P], ident, w.nzT_ps)

            def next_qk():
                e.wait_ge(w.nT_ok, 1)
                e.matmul(ps_s[:, 0, :], wq, nT[:, :], start=True, stop=True).then_inc(w.qkv_ps, 1)
                e.matmul(ps_s[:, 1, :], wk, nT[:, :], start=True, stop=True).then_inc(w.qkv_ps, 1)

            def next_v():
                for t in range(NT):
                    i = e.matmul(ps_s[:, 2, t * P:(t + 1) * P], nT[:, t * P:(t + 1) * P], wv, start=True, stop=True)
                i.then_inc(w.qkv_ps, 1)

            def unit(n):
                if n >= 2:
                    e.wait_ge(w.max_ok, n - 1)
                half, j = ORDER[n // 2] // HJ, ORDER[n // 2] % HJ
                for a in range(2):
                    t = 2 * (n % 2) + a
                    i = e.matmul(ps_s[:, t, :], q_st[:, half, j, t * P:(t + 1) * P], k_st[:, j, :],
                                 start=True, stop=True)
                i.then_inc(w.s1_ps, 1)

            def shift_rows(r):
                e.wait_ge(w.mp_ok, r + 1)
                e.wait_ge(w.h_ok, C0 * (r + 1))
                transposed(lambda t: mp[:, t, :], lambda t: ps_u16[0:PIECES * HJ, t * P:(t + 1) * P],
                           ident_b[:, :], w.mpt_ps)

            def second_product(bank, n, ex, t, weights, per):
                for c in range(per):
                    m = per * ex + c
                    i = e.matmul(bank[:, t * P:(t + 1) * P], hid[:, m, t * P:(t + 1) * P], weights[:, m, :],
                                 start=c == 0, stop=c == per - 1)
                if t == NT - 1:
                    i.then_inc(w.y_ps, 1)

            e.wait_ge(first_in, 16)
            next_T(False)
            next_qk()
            next_v()
            e.wait_ge(set_pe, 1)
            for c in range(CTX):
                i = e.matmul(ps_y[:, 0:G1], ones[:, :], w1g[:, c, 0:G1], start=c == 0, stop=c == CTX - 1)
            for c in range(CTX):
                e.matmul(ps_m[:, 0:G1], hid[:, 8, c * P:(c + 1) * P], w1m[:, c, :], start=c == 0, stop=False)
            e.matmul(ps_m[:, 0:G1], ones[0:1, :], rows_sb[:, 0:G1], start=False, stop=True)
            i = e.matmul(ps_m[:, G1:G1 + D], ones[0:1, :], rows_sb[:, G1:G1 + D], start=True, stop=True)
            i.then_inc(set_act, 1)
            e.wait_ge(v_in, 32)
            meet(e, "pe")

            with e.Fori(0, B):
                for loop in range(LOOPS):
                    if loop:
                        e.wait_ge(w.zs_ok, 1)
                    transposed(lambda t: zs[:, t, :], lambda t: ps_m[:, t * P:(t + 1) * P], ident, w.zT_ps)
                    e.wait_ge(w.xT_ok, loop + 1)
                    for t in range(NT):
                        i = e.matmul(ps_m[:, t * 12:(t + 1) * 12], xT[:, t * P:(t + 1) * P], wr,
                                     start=True, stop=True)
                    i.then_inc(w.lg_ps, 1)
                    e.wait_ge(w.hi_ok, loop + 1)
                    for i_ in range(C0):
                        n = C0 * loop + i_
                        if n >= 2:
                            e.wait_ge(w.h_ok, n - 1)
                        if loop and i_ == 0:
                            e.wait_ge(w.mpt_ok, 1)
                        u, cols = ps_u[:, i_ % 2, :], slice(i_ * P, (i_ + 1) * P)
                        e.matmul(u, w1_hi[:, cols], x_hi[:, :], start=True, stop=False)
                        e.matmul(u, w1_lo[:, cols], x_hi[:, :], start=False, stop=False)
                        if i_ == 0:
                            e.wait_ge(w.lo_ok, loop + 1)
                        e.matmul(u, w1_hi[:, cols], x_lo[:, :], start=False, stop=True).then_inc(w.u_ps, 1)
                        for m in after.get((loop, i_), ()):
                            unit(m)
                    for ex in range(E0):
                        e.wait_ge(w.h_ok, C0 * loop + 2 * ex + 2)
                        if ex == 1:
                            e.wait_ge(w.lg_ok, loop + 1)
                        if ex >= 2:
                            e.wait_ge(w.yc_ok, (E0 - 1) * loop + ex - 1)
                        for t in range(NT):
                            second_product(y_bank[ex % 2], loop, ex, t, w2_sb, 2)
                            if t % 2:
                                for m in after.get((loop, C0 + 2 * ex + t // 2), ()):
                                    unit(m)
                    if loop == 0:
                        shift_rows(0)

                def heads(g):
                    return [(0, 2 * g), (0, 2 * g + 1), (1, 2 * g), (1, 2 * g + 1)]

                def scores(v, pair):
                    g, kt = v // NT, v % NT
                    if v == 0:
                        e.wait_ge(w.max_ok, UNITS - 1 + pair)
                        e.wait_ge(w.shift_ok, 64)
                    else:
                        e.wait_ge(w.p_ok, 2 * (v - 1) + pair + 1)
                    if g == 2 and kt == 0:
                        e.wait_ge(w.shift_ok, 128)
                    for a in range(2):
                        half, j = heads(g)[2 * pair + a]
                        i = e.matmul(ps_s[:, 2 * pair + a, :], k_st[:, j, kt * P:(kt + 1) * P], q_st[:, half, j, :],
                                     start=True, stop=True)
                    i.then_inc(w.s2_ps, 1)

                def values(v):
                    g, kt = v // NT, v % NT
                    e.wait_ge(w.p_ok, 2 * v + 2)
                    if kt == 0:
                        if g >= 2:
                            e.wait_ge(w.o_ok, g - 1)
                        else:
                            e.wait_ge(w.mpt_ok, 2)
                    for a, (half, j) in enumerate(heads(g)):
                        i = e.matmul(ps_u[32 * a:32 * a + 32, g % 2, :], v_aug[:, kt * H + HJ * half + j, :],
                                     probs[:, v % 2, a, :], start=kt == 0, stop=kt == NT - 1,
                                     tile_position=(0, 32 * a))
                    i.then_inc(w.pv_ps, 1)

                def back(g):
                    e.wait_ge(w.o_ok, g + 1)
                    if g:
                        e.wait_ge(w.on_ok, g)
                    else:
                        e.wait_ge(w.z_ok, LOOPS)
                    transposed(lambda t: o_sb[:, t * P:(t + 1) * P], lambda t: ps_m[:, t * P:(t + 1) * P],
                               ident, w.oN_ps)

                scores(0, 0)
                scores(0, 1)
                shift_rows(1)
                for v in range(4 * NT):
                    if v + 1 < 4 * NT:
                        scores(v + 1, 0)
                        scores(v + 1, 1)
                    values(v)
                    if v % NT == 1 and v > NT:
                        back(v // NT - 1)
                next_T(True)
                back(3)
                next_qk()
                e.wait_ge(w.on_ok, 4)
                transposed(lambda t: on[:, t, :, :].rearrange("p g k -> p (g k)"),
                           lambda t: ps_m[:, t * P:(t + 1) * P], ident, w.onT_ps)
                next_v()
                e.wait_ge(w.hT_ok, 1)
                for t in range(NT):
                    i = e.matmul(ps_y[:, t * P:(t + 1) * P], hT[:, t * P:(t + 1) * P], wo, start=True, stop=True)
                i.then_inc(w.att_ps, 1)

                e.wait_ge(w.yn_ok, 1)
                transposed(lambda t: yn[:, t, :], lambda t: ps_m[:, t * P:(t + 1) * P], ident, w.zT_ps)
                e.wait_ge(w.xT_ok, LOOPS + 1)
                e.wait_ge(w.o_ok, 4)
                e.matmul(ps_u[:, 0, :], w_mag, xT[:, :], start=True, stop=True).then_inc(w.mq_ps, 1)
                e.matmul(ps_u[:, 1, :], w_q, xT[:, :], start=True, stop=True).then_inc(w.mq_ps, 1)
                for t in range(NT):
                    i = e.matmul(ps_m[:, t * E1:(t + 1) * E1], xT[:, t * P:(t + 1) * P], wr1,
                                 start=True, stop=True)
                i.then_inc(w.lg_ps, 1)
                e.wait_ge(w.hi_ok, LOOPS + 1)
                e.wait_ge(w.rest_ok, 2)
                e.wait_ge(w.part_ok, 2)
                for i_ in range(E1):
                    if i_ == 2:
                        e.wait_ge(w.v_ok, 1)
                    if i_ >= 4:
                        e.wait_ge(w.r_ok, i_ - 3)
                    u, cols = ps_s[:, i_ % 4, :], slice(i_ * P, (i_ + 1) * P)
                    e.matmul(u, v1_hi[:, cols], x_hi[:, :], start=True, stop=False)
                    e.matmul(u, v1_lo[:, cols], x_hi[:, :], start=False, stop=False)
                    if i_ == 0:
                        e.wait_ge(w.lo_ok, LOOPS + 1)
                    e.matmul(u, v1_hi[:, cols], x_lo[:, :], start=False, stop=True).then_inc(w.f_ps, 1)

                def second_of(ex):
                    e.wait_ge(w.a_ok, ex + 1)
                    if ex == 0:
                        e.wait_ge(w.x1_ok, 1)
                    if ex == 1:
                        e.wait_ge(w.sg_in, 1)
                    if ex >= 2:
                        e.wait_ge(w.yc_ok, (E0 - 1) * LOOPS + ex - 1)
                    for t in range(NT):
                        second_product(y_bank[ex % 2], LOOPS, ex, t, v2_sb, 1)

                for ex in range(E1):
                    second_of(ex)
                e.wait_ge(w.sq_ok, 3)
                e.wait_ge(w.ri_ok, 2)
                e.wait_ge(w.r_ok, E1)
                for t in range(NT):
                    for c in range(3):
                        i = e.matmul(ps_s[:, t, G1 + 1:G1 + 2], squares[:, c, t * P:(t + 1) * P],
                                     mean_col[:, :], start=c == 0, stop=c == 2)
                    for c in range(CTX):
                        i = e.matmul(ps_s[:, t, 0:G1 + 1], ctxt[:, c, t * P:(t + 1) * P], w1g[:, c, :],
                                     start=c == 0, stop=c == CTX - 1)
                i.then_inc(w.g_ps, 1)
                e.wait_ge(w.tg_ok, 1)
                e.wait_ge(w.ph_ok, 1)
                for t in range(NT):
                    e.wait_ge(w.ge_ok, t + 1)
                    for c in range(2):
                        i = e.transpose(ps_u[:, c, t * P:(t + 1) * P], ga[:, t, c * P:(c + 1) * P], ident)
                i.then_inc(w.gT_ps, 1)
                e.wait_ge(w.gT_ok, 1)
                e.wait_ge(w.yc_ok, (E0 - 1) * LOOPS + E1)
                for t in range(NT):
                    o = ps_m[:, t * P:(t + 1) * P]
                    for c in range(2):
                        i = e.matmul(o, gT[:, c, t * P:(t + 1) * P], w2m[:, c, :], start=c == 0, stop=c == 1)
                i.then_inc(w.mlp_ps, 1)
                meet(e, "pe")

        @block.scalar
        def _(e):
            a = e.activation

            def next_first():
                e.wait_ge(w.nzT_ps, 1)
                e.copy(nT[:, :], ps_s[:, 3, :]).then_inc(w.nT_ok, 1)
                for which in range(2):
                    e.wait_ge(w.qkv_ps, which + 1)
                    e.copy(parts[:, which, 0, :], ps_s[:, which, :]).then_inc(w.part_ok, 1)

            def next_second():
                for which in range(2):
                    e.wait_ge(w.rest_ok, which + 1)
                    e.copy(parts[:, which, 1, :], rest[:, which, :]).then_inc(w.part_ok, 1)

            def weighted(n, ex, dst):
                e.wait_ge(w.y_ps, E0 * n + ex + 1)
                for t in range(NT):
                    i = a(dst[:, t, :], y_bank[ex % 2][:, t * P:(t + 1) * P], ACT.Copy, scale=cw[:, t, ex:ex + 1])
                i.then_inc(w.yc_ok, 1)

            next_first()
            next_second()
            e.wait_ge(set_up, 8)
            a(sin_phi[:, :], ws[:, :], ACT.Sin)
            a(cos_phi[:, :], ph_abs, ACT.Sin, bias=half_pi[:, :], scale=-1.0)
            e.wait_ge(set_act, 1)
            e.copy(b1_all[:, :], ps_m[:, 0:G1])
            e.copy(b2_all[:, :], ps_m[:, G1:G1 + D])
            meet(e, "act")

            with e.Fori(0, B):
                for loop in range(LOOPS):
                    e.wait_ge(w.zT_ps, loop + 1)
                    a(xT[:, :], ps_m[:, :], ACT.Copy, scale=f_("norm_w")).then_inc(w.xT_ok, 1)
                    for i in range(C0):
                        if i == 4:
                            e.wait_ge(w.lt_in, loop + 1)
                            a(lt[:, :, :], ld[:, :, :], ACT.Tanh, scale=0.5).then_inc(w.lt_ok, 1)
                        e.wait_ge(w.u_ps, C0 * loop + i + 1)
                        a(hid[:, i, :], ps_u[:, i % 2, :], ACT.Silu).then_inc(w.h_ok, 1)
                    e.wait_ge(w.cw_ok, loop + 1)
                    for ex in range(E0 - 1):
                        n = (E0 - 1) * loop + ex
                        if n >= 2:
                            e.wait_ge(w.za_ok, n - 1)
                        weighted(loop, ex, part_y[:, n % 2])
                    if loop == LOOPS - 1:
                        e.wait_ge(w.z_ok, LOOPS)
                        a(gate[:, :, :], z[:, :, :], ACT.Silu).then_inc(w.gate_ok, 1)
                    e.wait_ge(w.mpt_ps, loop + 1)
                    if loop:
                        e.wait_ge(w.m_out, 16)
                    e.copy(mpt[:, :], ps_u16[0:PIECES * HJ, 0:S]).then_inc(w.mpt_ok, 1)
                for v in range(4 * NT):
                    if v >= 2:
                        e.wait_ge(w.pv_ps, v - 1)
                    for pair in range(2):
                        e.wait_ge(w.s2_ps, 2 * v + pair + 1)
                        a(probs[:, v % 2, 2 * pair:2 * pair + 2, :], ps_s[:, 2 * pair:2 * pair + 2, :], ACT.Exp,
                          scale=float(HD) ** -0.5).then_inc(w.p_ok, 1)
                next_first()
                e.wait_ge(w.onT_ps, 1)
                e.copy(hT[:, :], ps_m[:, :]).then_inc(w.hT_ok, 1)
                next_second()
                e.wait_ge(w.zT_ps, LOOPS + 1)
                e.copy(xT[:, :], ps_m[:, :]).then_inc(w.xT_ok, 1)
                e.wait_ge(w.mq_ps, 1)
                a(tg, ps_u[:, 0, :], ACT.Tanh, bias=b_mag_half[:, :], scale=0.5).then_inc(w.tg_ok, 1)
                a(squares[:, 2, :], xT[:, :], ACT.Square).then_inc(w.sq_ok, 1)

                def relu(i):
                    e.wait_ge(w.f_ps, i + 1)
                    a(hid[:, i, :], ps_s[:, i % 4, :], ACT.Relu).then_inc(w.r_ok, 1)

                for i in range(4):
                    relu(i)
                e.wait_ge(w.ph_ok, 2)
                a(sq, phq, ACT.Sin).then_inc(w.sc_ok, 1)
                a(cq, ph_abs, ACT.Sin, bias=half_pi[:, :], scale=-1.0).then_inc(w.sc_ok, 1)
                e.wait_ge(w.acc_ok, 1)
                a(acc[:, :], acc[:, :], ACT.Sqrt, bias=tiny[:, :], scale=MAG).then_inc(w.inv_in, 1)
                for i in range(4, E1):
                    relu(i)
                for c in range(2):
                    e.wait_ge(w.mem_ok, c + 1)
                    a(squares[:, c, :], mem[:, c, :], ACT.Square).then_inc(w.sq_ok, 1)
                e.wait_ge(w.cw_ok, LOOPS + 1)
                e.wait_ge(w.x1_ok, 1)
                base = (E0 - 1) * LOOPS
                for ex in range(E1):
                    n = base + ex
                    if ex:
                        e.wait_ge(w.za_ok, base if ex < 3 else n - 2)
                    weighted(LOOPS, ex, part_y[:, n % 2] if ex else gate)
                e.wait_ge(w.za_ok, base + E1 - 1)
                a(gate[:, :, :], gate[:, :, :], ACT.Silu).then_inc(w.gate_ok, 1)
                for t in range(NT):
                    e.wait_ge(w.ga_ok, t + 1)
                    a(ga[:, t, :], ga[:, t, :], ACT.Gelu).then_inc(w.ge_ok, 1)
                e.wait_ge(w.gT_ps, 1)
                e.copy(gT[:, :, :], ps_u[:, :, :]).then_inc(w.gT_ok, 1)
                meet(e, "act")

        @block.gpsimd
        def _(e):
            count = [0]

            def link(ins):
                count[0] += 1
                ins.then_inc(w.pool, 1)
                e.wait_ge(w.pool, count[0])

            def power(dst, src, scale, eps, done):
                link(e.tensor_scalar(dst, src, scale, eps, ALU.mult, ALU.add))
                e.tensor_tensor(dst, dst, minus_half[:, :], ALU.pow).then_inc(done, 1)

            def next_norms():
                e.wait_ge(w.nstats_ok, 1)
                power(rstd_n[:, :], mv_n[:, :, 1], 1.0, 1e-5, w.nrstd_ok)
                e.wait_ge(w.nssq_ok, 1)
                power(rstd_n[:, :], ssq[:, :], 1.0 / D, 1e-6, w.nrstd_ok)

            e.memset(q_st[:, :, :, :], 0.0).then_inc(set_pool, 1)
            e.wait_ge(set_up, 1)
            next_norms()
            meet(e, "pool")
            with e.Fori(0, B):
                count[0] = 0
                e.tensor_copy(xin[:, :, :], x_next[:, :, :]).then_inc(w.x_used, 1)

                def accumulate(n, ex, dst, last_in):
                    e.wait_ge(w.yc_ok, n + 1)
                    link_in = e.tensor_tensor(dst[:, :, :], dst[:, :, :], part_y[:, n % 2], ALU.add)
                    link_in.then_inc(w.za_ok, 1)

                for loop in range(LOOPS):
                    if loop:
                        e.wait_ge(w.ssq_ok, 1)
                        power(rstd[:, :], ssq[:, :], 1.0 / D, 1e-6, w.rstd_ok)
                        e.wait_ge(w.zs_ok, 1)
                    for ex in range(E0 - 1):
                        n = (E0 - 1) * loop + ex
                        if ex:
                            e.wait_ge(w.za_ok, n)
                        accumulate(n, ex, z, n)
                next_norms()
                e.wait_ge(w.stats_ok, 1)
                power(rstd[:, :], mv[:, :, 1], 1.0, 1e-5, w.rstd_ok)
                e.wait_ge(w.xT_ok, LOOPS + 1)
                e.tensor_tensor(ctxt[:, 0, :], xT[:, :], cos_phi[:, :], ALU.mult).then_inc(w.c01_ok, 1)
                e.wait_ge(w.sg_in, 1)
                e.tensor_tensor(le[:, :, 0:E1], euler[:, :].rearrange("p (t x) -> p t x", t=NT),
                                ld[:, :, 0:E1], ALU.pow).then_inc(w.sg_ok, 1)
                e.tensor_tensor(ctxt[:, 1, :], xT[:, :], sin_phi[:, :], ALU.mult).then_inc(w.c01_ok, 1)
                e.tensor_tensor(yn[:, :, :], yn[:, :, :], b2_all[:, :].unsqueeze(1).to_broadcast([P, NT, D]), ALU.add
                                ).then_inc(w.ynb_ok, 1)
                e.wait_ge(w.mem_ok, 1)
                e.wait_ge(w.sc_ok, 2)
                e.tensor_tensor(wc, mem_r, cq, ALU.mult).then_inc(w.rot_in, 1)
                e.tensor_tensor(ws[:, :], mem_r, sq, ALU.mult).then_inc(w.rot_in, 1)
                base = (E0 - 1) * LOOPS
                for ex in range(1, E1):
                    n = base + ex
                    e.wait_ge(w.yc_ok, n + 1)
                    if ex > 1:
                        e.wait_ge(w.za_ok, n - 1)
                    e.tensor_tensor(gate[:, :, :], gate[:, :, :], part_y[:, n % 2], ALU.add).then_inc(w.za_ok, 1)
                e.wait_ge(w.var_ok, 1)
                power(rstd[:, :], var[:, :], 1.0, 1e-5, w.rstd_ok)
                meet(e, "pool")

        @block.vector
        def _(e):
            setup = [0]

            def step(ins):
                setup[0] += 1
                ins.then_inc(set_up, 1)
                e.wait_ge(set_up, setup[0])

            tt, ts, stt = e.tensor_tensor, e.tensor_scalar, e.scalar_tensor_tensor

            count = [0]

            def link(ins):
                count[0] += 1
                ins.then_inc(w.dve, 1)
                e.wait_ge(w.dve, count[0])

            def reduce_turns(chain, x_, t_):
                chain(ts(t_, x_, float(1 / (2 * np.pi)), ROUND, ALU.mult, ALU.add))
                chain(ts(t_, t_, ROUND, None, ALU.subtract))
                chain(stt(x_, t_, -TWO_PI_A, x_, ALU.mult, ALU.add))
                chain(stt(x_, t_, -TWO_PI_B, x_, ALU.mult, ALU.add))

            def norm_stats(src, bn, m, done):
                for t in range(NT):
                    i = e.bn_stats(bn[:, t, :], src[:, t, :])
                link(i)
                for t in range(NT):
                    i = e.bn_aggr(m[:, t, :], bn[:, t, :])
                i.then_inc(done, 1)

            def norm_apply(src, dst, m, r, done):
                for t in range(NT):
                    i = ts(dst[:, t, :], src[:, t, :], m[:, t, 0:1], r[:, t:t + 1], ALU.subtract, ALU.mult)
                i.then_inc(done, 1)

            def sum_squares(done):
                for t in range(NT):
                    i = e.tensor_tensor_reduce(zs[:, t, :], z[:, t, :], z[:, t, :], 1.0, 0.0, ALU.mult,
                                               ALU.add, ssq[:, t:t + 1])
                i.then_inc(done, 1)

            def rms_apply(r, done):
                for t in range(NT):
                    i = ts(zs[:, t, :], z[:, t, :], r[:, t:t + 1], None, ALU.mult)
                i.then_inc(done, 1)

            def next_norms():
                e.wait_ge(x_in, 16)
                e.nop().then_inc(x_in, -16)
                norm_stats(x_next, bn6_n, mv_n, w.nstats_ok)
                e.wait_ge(w.nrstd_ok, 1)
                norm_apply(x_next, z, mv_n, rstd_n, w.nz_ok)
                e.wait_ge(w.nz_ok, 1)
                sum_squares(w.nssq_ok)
                e.wait_ge(w.nrstd_ok, 2)
                rms_apply(rstd_n, w.nzs_ok)

            def next_rest():
                for which in range(2):
                    e.wait_ge(w.part_ok, which + 1)
                    tt(rest[:, which, :], ps_s[:, which, :], parts[:, which, 0, :], ALU.subtract
                       ).then_inc(w.rest_ok, 1)

            def next_third():
                for which in range(2):
                    e.wait_ge(w.part_ok, which + 3)
                    tt(parts[:, which, 2, :], rest[:, which, :], parts[:, which, 1, :], ALU.subtract
                       ).then_inc(w.parts_ok, 1)

            def next_v():
                e.wait_ge(w.qkv_ps, 3)
                e.tensor_copy(v_aug[:, :, 0:HD], ps_s[:, 2, :].rearrange("p (a v) -> p a v", v=HD)
                              ).then_inc(w.v_ok, 1)

            for tile, value in ((minus_half, -0.5), (half_pi, float(np.pi / 2)), (tiny, 1e-8),
                                (euler, float(np.e)), (mean_col, 1.0 / (CTX * P)), (ones, 1.0), (ones_row, 1.0)):
                i = e.memset(tile[:, :], value)
            step(i)
            next_norms()
            e.wait_ge(first_in, 16)
            step(ts(phi[:, :], f_("pos"), f_("phases"), 0.01, ALU.mult, ALU.mult))
            step(e.tensor_copy(ws[:, :], phi[:, :]))
            reduce_turns(step, ws[:, :], wc)
            e.memset(v_aug[:, :, :], 0.0)
            e.memset(k_st[:, :, :], 1.0)
            e.tensor_copy(ident_b[:, :], ident)
            next_rest()
            next_third()
            stt(ph_abs, ws[:, :], -1.0, ws[:, :], ALU.mult, ALU.max)
            step(ts(ws[:, :], ws[:, :], PI_BELOW, -PI_BELOW, ALU.min, ALU.max))
            step(e.memset(v_aug[:, :, HD:HD + 1], 1.0))
            next_v()
            e.wait_ge(second_in, 32)
            for c in range(CTX):
                ts(w1g[:, c, 0:G1], w1m[:, c, :], f_("ln_g")[:, c:c + 1], None, ALU.mult)
                ts(hid[:, 8, c * P:(c + 1) * P], ones[:, :], f_("ln_b")[:, c:c + 1], None, ALU.mult)
                e.memset(w1g[:, c, G1:G1 + 1], 1.0 / (CTX * P))
            e.tensor_scalar(b_mag_half[:, :], f_("b_mag"), 0.5, None, ALU.mult).then_inc(set_pe, 1)
            e.wait_ge(w_in, 32)
            wv1 = hid[:, 0:4, :].rearrange("p a n -> p (a n)")
            vv1 = hid[:, 4:6, :].rearrange("p a n -> p (a n)")
            e.tensor_copy(w1_hi[:, :], wv1)
            step(e.tensor_copy(v1_hi[:, :], vv1))
            tt(w1_lo[:, :], wv1, w1_hi[:, :].bitcast(F32), ALU.subtract)
            step(tt(v1_lo[:, :], vv1, v1_hi[:, :].bitcast(F32), ALU.subtract))
            e.wait_ge(set_act, 1)
            for c in range(CTX):
                i = stt(w1g[:, c, 0:G1], ps_y[:, 0:G1], -1.0 / (CTX * P), w1g[:, c, 0:G1], ALU.mult, ALU.add)
            meet(e, "dve")

            def split_x(n):
                e.wait_ge(w.xT_ok, n)
                e.tensor_copy(x_hi[:, :], xT[:, :]).then_inc(w.hi_ok, 1)
                e.wait_ge(w.hi_ok, n)
                tt(x_lo[:, :], xT[:, :], x_hi[:, :].bitcast(F32), ALU.subtract).then_inc(w.lo_ok, 1)

            def rank_of(p, n, mask):
                sh = [P, NT, n, n]
                mine = p.unsqueeze(3).to_broadcast(sh)
                theirs = p.unsqueeze(2).to_broadcast(sh)
                b4 = beat[:, 0:NT * n * n].rearrange("p (t i j) -> p t i j", t=NT, i=n)
                t4 = tie[:, 0:NT * n * n].rearrange("p (t i j) -> p t i j", t=NT, i=n)
                tt(b4, theirs, mine, ALU.is_gt)
                link(tt(t4, theirs, mine, ALU.is_equal))
                link(tt(t4, t4, mask, ALU.mult))
                link(tt(b4, b4, t4, ALU.add))
                rk = rank[:, 0:NT * n].rearrange("p (t i) -> p t i", t=NT)
                link(e.tensor_reduce(rk, b4, AX.X, ALU.add))
                return rk

            def bcast(v, n):
                return v.unsqueeze(2).to_broadcast([P, NT, n])

            low4 = lower[:, 0:16].rearrange("p (i j) -> p i j", i=4)
            low8 = lower[:, 64:128].rearrange("p (i j) -> p i j", i=8)

            def router0_a(loop):
                e.wait_ge(w.lg_ps, loop + 1)
                e.tensor_copy(lg[:, :, :], ps_m[:, 0:NT * 12].rearrange("p (t x) -> p t x", t=NT)
                              ).then_inc(w.lg_ok, 1)
                e.wait_ge(w.lg_ok, loop + 1)
                pair = lg[:, :, 4:12].rearrange("p t (g e) -> p t g e", e=2)
                e.tensor_reduce(lm[:, :, 0:1], lg[:, :, 0:4], AX.X, ALU.max)
                link(e.tensor_reduce(lm[:, :, 1:5], pair, AX.X, ALU.max))
                tt(ld[:, :, 0:4], lg[:, :, 0:4], lm[:, :, 0:1].to_broadcast([P, NT, 4]), ALU.subtract)
                tt(ld[:, :, 4:12].rearrange("p t (g e) -> p t g e", e=2), pair,
                   lm[:, :, 1:5].unsqueeze(3).to_broadcast([P, NT, 4, 2]), ALU.subtract).then_inc(w.lt_in, 1)

            def router0_b(loop):
                e.wait_ge(w.lt_ok, loop + 1)
                link(ts(ld[:, :, :], lt[:, :, :], -1.0, 1.0, ALU.mult, ALU.add))
                link(e.reciprocal(ld[:, :, :], ld[:, :, :]))
                link(stt(le[:, :, :].rearrange("p t x -> p (t x)"), lt[:, :, :].rearrange("p t x -> p (t x)"), 1.0,
                         ld[:, :, :].rearrange("p t x -> p (t x)"), ALU.add, ALU.mult))
                pair = le[:, :, 4:12].rearrange("p t (g e) -> p t g e", e=2)
                e.tensor_reduce(lm[:, :, 0:1], le[:, :, 0:4], AX.X, ALU.add)
                link(e.tensor_reduce(lm[:, :, 1:5], pair, AX.X, ALU.add))
                link(e.reciprocal(lm[:, :, :], lm[:, :, :]))
                tt(le[:, :, 0:4], le[:, :, 0:4], lm[:, :, 0:1].to_broadcast([P, NT, 4]), ALU.mult)
                link(tt(pair, pair, lm[:, :, 1:5].unsqueeze(3).to_broadcast([P, NT, 4, 2]), ALU.mult))
                rk = rank_of(lg[:, :, 0:4], 4, low4.unsqueeze(1).to_broadcast([P, NT, 4, 4]))
                link(stt(gw[:, :, :], rk, 1.5, le[:, :, 0:4], ALU.is_lt, ALU.mult))
                link(e.tensor_reduce(wsum[:, :], gw[:, :, :], AX.X, ALU.add))
                link(ts(wsum[:, :], wsum[:, :], 1e-9, None, ALU.add))
                link(e.reciprocal(wsum[:, :], wsum[:, :]))
                tt(gw[:, :, :], gw[:, :, :], bcast(wsum[:, :], 4), ALU.mult)
                link(e.tensor_reduce(lm[:, :, 1:5], pair, AX.X, ALU.max))
                link(ts(ld[:, :, 0:4], lm[:, :, 1:5], 1e-9, None, ALU.add))
                link(e.reciprocal(ld[:, :, 0:4], ld[:, :, 0:4]))
                link(tt(lm[:, :, 1:5], lm[:, :, 1:5], ld[:, :, 0:4], ALU.mult))
                tt(gw[:, :, :], gw[:, :, :], lm[:, :, 1:5], ALU.mult)
                link(tt(ld[:, :, 4:8], pair[:, :, :, 0], pair[:, :, :, 1], ALU.is_ge))
                cwp = cw[:, :, :].rearrange("p t (g e) -> p t g e", e=2)
                link(tt(cwp[:, :, :, 0], ld[:, :, 4:8], gw[:, :, :], ALU.mult))
                tt(cwp[:, :, :, 1], gw[:, :, :], cwp[:, :, :, 0], ALU.subtract).then_inc(w.cw_ok, 1)

            def max_of(n):
                e.wait_ge(w.s1_ps, n + 1)
                t = 2 * (n % 2)
                e.tensor_reduce(smax[:, t:t + 2, n // 2], ps_s[:, t:t + 2, :], AX.X, ALU.max).then_inc(w.max_ok, 1)

            def negated_maxima(r):
                e.wait_ge(w.max_ok, ROUND_UNITS * (r + 1))
                if r:
                    e.wait_ge(w.mpt_ps, r)
                sm = smax[:, :, HJ * r:HJ * (r + 1)]
                link(ts(mp[:, :, 0:HJ], sm, -1.0, None, ALU.mult))
                link(stt(mrest[:, :, :], sm, -1.0, mp[:, :, 0:HJ], ALU.mult, ALU.subtract))
                link(e.tensor_copy(mp[:, :, HJ:2 * HJ], mrest[:, :, :]))
                tt(mp[:, :, 2 * HJ:3 * HJ], mrest[:, :, :], mp[:, :, HJ:2 * HJ], ALU.subtract
                   ).then_inc(w.mp_ok, 1)

            with e.Fori(0, B):
                count[0] = 0
                for loop in range(LOOPS):
                    split_x(loop + 1)
                    router0_a(loop)
                    router0_b(loop)
                    for n in range(ROUND_UNITS * loop, ROUND_UNITS * (loop + 1)):
                        max_of(n)
                    e.wait_ge(w.y_ps, E0 * (loop + 1))
                    e.wait_ge(w.za_ok, (E0 - 1) * (loop + 1))
                    e.wait_ge(w.cw_ok, loop + 1)
                    for t in range(NT):
                        i = stt(z[:, t, :], y_bank[(E0 - 1) % 2][:, t * P:(t + 1) * P], cw[:, t, E0 - 1:E0], z[:, t, :],
                                ALU.mult, ALU.add)
                    i.then_inc(w.z_ok, 1)
                    e.wait_ge(w.z_ok, loop + 1)
                    if loop == 0:
                        sum_squares(w.ssq_ok)
                    negated_maxima(loop)
                    if loop == 0:
                        e.wait_ge(w.rstd_ok, 1)
                        rms_apply(rstd, w.zs_ok)
                for g in range(4):
                    e.wait_ge(w.pv_ps, NT * (g + 1))
                    if g:
                        e.wait_ge(w.oN_ps, g)
                    e.tensor_copy(o_sb[:, :], ps_u[:, g % 2, :]).then_inc(w.o_ok, 1)
                    e.wait_ge(w.oN_ps, g + 1)
                    src = ps_m[:, :].rearrange("p (a k) -> p a k", k=32)
                    link(e.reciprocal(oden[:, :, :], src[:, :, HD:HD + 1]))
                    dst = on[:, :, g, :].rearrange("p t (a v) -> p t a v", v=HD)
                    tt(dst, ps_m[:, :].rearrange("p (t a k) -> p t a k", t=NT, k=32)[:, :, :, 0:HD],
                       oden[:, :, 0].rearrange("p (t a) -> p t a", t=NT).unsqueeze(3).to_broadcast([P, NT, 4, HD]),
                       ALU.mult).then_inc(w.on_ok, 1)
                    if g == 0:
                        e.wait_ge(w.gate_ok, 1)
                        next_norms()
                next_rest()
                flat = lambda v: v[:, :, :].rearrange("p t d -> p (t d)")
                x1f, xf, ynf, of, gf = flat(x1), flat(xin), flat(yn), flat(outb), flat(gate)
                e.wait_ge(w.att_ps, 1)
                e.wait_ge(w.x_used, 1)
                link(tt(x1f, ps_y[:, :], gf, ALU.mult))
                tt(x1f, x1f, xf, ALU.add).then_inc(w.x1_ok, 1)
                e.wait_ge(w.x1_ok, 1)
                norm_stats(x1, bn6, mv, w.stats_ok)
                next_third()
                e.wait_ge(w.rstd_ok, 2)
                norm_apply(x1, yn, mv, rstd, w.yn_ok)
                next_v()

                split_x(LOOPS + 1)
                e.wait_ge(w.mq_ps, 2)
                stt(phq, ps_u[:, 1, :], f_("b_q"), phi[:, :], ALU.add, ALU.add).then_inc(w.ph_ok, 1)
                e.wait_ge(w.ph_ok, 1)
                e.wait_ge(w.lg_ps, LOOPS + 1)
                ts(ld[:, :, 0:E1], ps_m[:, 0:NT * E1].rearrange("p (t x) -> p t x", t=NT), -1.0, None, ALU.mult
                   ).then_inc(w.sg_in, 1)
                reduce_turns(link, phq, turns)
                stt(ph_abs, phq, -1.0, phq, ALU.mult, ALU.max)
                ts(phq, phq, PI_BELOW, -PI_BELOW, ALU.min, ALU.max).then_inc(w.ph_ok, 1)
                e.wait_ge(w.tg_ok, 1)
                e.tensor_tensor_scan(acc[:, :], tg, ones_row[:, :], 0.0, ALU.add, ALU.add
                                     ).then_inc(w.acc_ok, 1)

                def squared(i):
                    e.wait_ge(w.r_ok, i + 1)
                    tt(hid[:, i, :], hid[:, i, :], hid[:, i, :], ALU.mult).then_inc(w.a_ok, 1)

                squared(0)
                squared(1)
                link(stt(wgt, tg, 1.0, xT[:, :], ALU.add, ALU.mult))
                tt(wc, wgt, cos_phi[:, :], ALU.mult)
                link(tt(ws[:, :], wgt, sin_phi[:, :], ALU.mult))
                squared(2)
                squared(3)
                e.tensor_tensor_scan(mem_r, ones_row[:, :], wc, 0.0, ALU.mult, ALU.add)
                link(e.tensor_tensor_scan(mem_i, ones_row[:, :], ws[:, :], 0.0, ALU.mult, ALU.add))
                e.wait_ge(w.inv_in, 1)
                link(e.reciprocal(inv[:, :], acc[:, :]))
                stt(mem_r, mem_r, MAG, inv[:, :], ALU.mult, ALU.mult).then_inc(w.mem_ok, 1)
                stt(mem_i, mem_i, MAG, inv[:, :], ALU.mult, ALU.mult).then_inc(w.mem_ok, 1)
                for i in range(4, E1):
                    squared(i)
                e.wait_ge(w.sc_ok, 2)
                e.wait_ge(w.mem_ok, 2)
                tt(turns, mem_i, sq, ALU.mult)
                e.wait_ge(w.sq_ok, 3)
                link(tt(mem_i, mem_i, cq, ALU.mult))
                e.wait_ge(w.rot_in, 2)
                tt(ctxt[:, 2, :], wc, turns, ALU.add).then_inc(w.ri_ok, 1)
                tt(ctxt[:, 3, :], mem_i, ws[:, :], ALU.subtract).then_inc(w.ri_ok, 1)
                e.wait_ge(w.sg_ok, 1)
                link(ts(le[:, :, 0:E1], le[:, :, 0:E1], 1.0, None, ALU.add))
                link(e.reciprocal(lg[:, :, 0:E1], le[:, :, 0:E1]))
                rk = rank_of(lg[:, :, 0:E1], E1, low8.unsqueeze(1).to_broadcast([P, NT, E1, E1]))
                link(stt(cw[:, :, :], rk, 1.5, lg[:, :, 0:E1], ALU.is_lt, ALU.mult))
                link(e.tensor_reduce(wsum[:, :], cw[:, :, :], AX.X, ALU.add))
                link(ts(wsum[:, :], wsum[:, :], 1e-20, None, ALU.add))
                link(e.reciprocal(wsum[:, :], wsum[:, :]))
                tt(cw[:, :, :], cw[:, :, :], bcast(wsum[:, :], E1), ALU.mult).then_inc(w.cw_ok, 1)
                e.wait_ge(w.g_ps, 1)
                link(e.tensor_copy(stat[:, :, :], ps_s[:, :, G1:G1 + 2]))
                link(tt(var[:, :], stat[:, :, 0], stat[:, :, 0], ALU.mult))
                tt(var[:, :], stat[:, :, 1], var[:, :], ALU.subtract).then_inc(w.var_ok, 1)
                e.wait_ge(w.rstd_ok, 3)
                for t in range(NT):
                    stt(ga[:, t, :], ps_s[:, t, 0:G1], rstd[:, t:t + 1], b1_all[:, :], ALU.mult, ALU.add
                        ).then_inc(w.ga_ok, 1)
                e.wait_ge(stored, 16)
                e.nop().then_inc(stored, -16)
                e.wait_ge(w.mlp_ps, 1)
                e.wait_ge(w.ynb_ok, 1)
                link(tt(of, ps_m[:, :], ynf, ALU.add))
                e.wait_ge(w.gate_ok, 2)
                link(tt(of, of, gf, ALU.mult))
                tt(of, of, x1f, ALU.add).then_inc(w.out_ok, 1)
                meet(e, "dve")


_INPUTS = ("x", "first", "second", "w1", "w2", "v1", "v2", "rows")


def _layouts(i):
    a = {k: np.asarray(v) for k, v in i.items()}
    by_half = lambda v: v.reshape(2, HJ, D, HD).transpose(2, 0, 3, 1).reshape(D, D)
    column = lambda v: v.reshape(-1, P).T
    first = dict(
        ident=np.eye(P, dtype=np.float32),
        wq=by_half(a["L0_attn_W_query"]),
        wk=by_half(a["L0_attn_W_key"]),
        wv=a["L0_attn_W_val"].transpose(1, 0, 2).reshape(D, D),
        wr=np.concatenate([a["L0_ffn_w_macro"], a["L0_ffn_w_micro"].reshape(E0, D)]).T,
        norm_w=column(a["L0_ffn_norm_w"]),
        phases=column(a["L1_attn_random_phases"]),
        b_mag=column(a["L1_attn_b_mag"]),
        b_q=column(a["L1_attn_b_q"]),
        ln_g=column(a["L1_attn_ln_g"]),
        ln_b=column(a["L1_attn_ln_b"]),
        pos=np.broadcast_to(np.arange(S, dtype=np.float32), (P, S)),
    )
    return a, first, column


def kernel(**inputs):
    import concourse.bacc as bacc
    from concourse.bass_utils import run_bass_kernel_spmd as run

    a, first, column = _layouts(inputs)
    low = np.zeros((P, 2, 64), np.float32)
    low[:, 0, :16] = np.tril(np.ones((4, 4), np.float32), -1).ravel()
    low[:, 1, :] = np.tril(np.ones((8, 8), np.float32), -1).ravel()
    first["lower"] = low.reshape(P, 128)
    second = dict(
        wo=a["L0_attn_W_out"].reshape(2, 4, 2, HD, D).transpose(1, 0, 2, 3, 4).reshape(D, D),
        w_mag=a["L1_attn_W_mag"].T,
        w_q=a["L1_attn_W_q"].T,
        w2m=a["L1_attn_W2"].reshape(D, 2, P).transpose(2, 1, 0).reshape(P, G1),
        wr1=a["L1_ffn_router_w"].T,
        w1m=a["L1_attn_W1"].reshape(G1, CTX, P).transpose(2, 1, 0).reshape(P, CTX * G1),
    )
    arrays = dict(
        x=a["L0_attn_q"],
        first=np.concatenate([first[n] for n in FIRST], axis=1),
        second=np.concatenate([second[n] for n in SECOND], axis=1),
        w1=a["L0_ffn_w1"].reshape(E0 * F0, D).T,
        w2=a["L0_ffn_w2"].reshape(E0, D, 2, P).transpose(3, 0, 2, 1).reshape(P, C0 * D),
        v1=a["L1_ffn_w1"],
        v2=a["L1_ffn_w2"].reshape(E1, P, D).transpose(1, 0, 2).reshape(P, E1 * D),
        rows=np.concatenate([a["L1_attn_b1"], a["L1_attn_b2"]])[None, :],
    )
    nc = bacc.Bacc("TRN2", target_bir_lowering=False, num_devices=1)
    args, sent = [], {}
    for name in _INPUTS:
        v = np.ascontiguousarray(arrays[name])
        sent[f"in_{name}"] = v
        args.append(nc.dram_tensor(f"in_{name}", v.shape, mybir.dt.from_np(v.dtype), kind="ExternalInput").ap())
    args.append(nc.dram_tensor("out_0", (B, S, D), F32, kind="ExternalOutput").ap())
    build(nc, *args)
    return run(nc, [sent], core_ids=[0]).results[0]["out_0"]
```

```python
from contextlib import ExitStack

import numpy as np

import concourse.bass as bass
from concourse import mybir

F32 = mybir.dt.float32
F32R = mybir.dt.float32r
BF16 = mybir.dt.bfloat16
ALU = mybir.AluOpType
ACT = mybir.ActivationFunctionType
AX = mybir.AxisListType

P = 128
B, S, D = 8, 512, 128
NT = S // P
H, HD = 16, 8
HJ = H // 2
PIECES = 3
Q_PART = (0, 0, 0, 1, 1, 2)
K_PART = (0, 1, 2, 0, 1, 0)
ROWS = len(Q_PART) * HD
STACK_Q = ((0, 0, 0, 3), (3 * HD, 1, 0, 2), (5 * HD, 2, 0, 1))
STACK_K = ((0, 0, 1, 3), (3 * HD, 0, 1, 2), (5 * HD, 0, 0, 1))
STACK_DMAS = 2 * (len(STACK_Q) + len(STACK_K)) + 2
E0, F0 = 8, 256
C0 = E0 * F0 // P
LOOPS = 2
GROUPS = 4
E1 = 8
G1 = 2 * D
CTX = 4
ROUND = float(1.5 * 2 ** 23)
TWO_PI_A = 6.28125
TWO_PI_B = float(2 * np.pi - 6.28125)
PI_BELOW = 3.1415925
MAG = 2.5

FIRST = dict(ident=128, wq=128, wk=128, wv=128, wr=GROUPS + E0, norm_w=1, phases=1, b_mag=1, b_q=1,
             ln_g=CTX, ln_b=CTX, lower=128, pos=S)
SECOND = dict(wo=128, w_mag=128, w_q=128, w2m=G1, wr1=E1, w1m=CTX * G1)


def columns(widths, name):
    at = 0
    for n, w in widths.items():
        if n == name:
            return slice(at, at + w)
        at += w


def build(nc, x, first, second, w1, w2, v1, v2, rows, out):
    ctx = ExitStack()
    with ctx:
        def sb(name, shape, dt=F32):
            return ctx.enter_context(nc.sbuf_tensor(name, shape, dt))

        def psum(name, shape, dt=F32):
            return ctx.enter_context(nc.psum_tensor(name, shape, dt))

        c_first = sb("c_first", [P, sum(FIRST.values())])
        c_second = sb("c_second", [P, sum(SECOND.values())])

        def f_(name):
            return c_first[:, columns(FIRST, name)]

        def g_(name):
            return c_second[:, columns(SECOND, name)]

        ident, wq, wk, wv, wr = f_("ident"), f_("wq"), f_("wk"), f_("wv"), f_("wr")
        lower = f_("lower")
        wo, w_mag, w_q, wr1 = g_("wo"), g_("w_mag"), g_("w_q"), g_("wr1")
        w2m = g_("w2m").rearrange("p (c d) -> p c d", c=2)
        w1m = g_("w1m").rearrange("p (c g) -> p c g", c=CTX)
        w1_hi, w1_lo = sb("w1_hi", [P, C0 * P], F32R), sb("w1_lo", [P, C0 * P], F32R)
        v1_hi, v1_lo = sb("v1_hi", [P, E1 * P], F32R), sb("v1_lo", [P, E1 * P], F32R)
        w2_sb, v2_sb = sb("w2_sb", [P, C0, D]), sb("v2_sb", [P, E1, D])
        rows_sb = sb("rows_sb", [1, G1 + D])
        ident_b = sb("ident_b", [P, P], BF16)
        ones = sb("ones", [P, P])
        ones_row = sb("ones_row", [P, S])
        mean_col = sb("mean_col", [P, 1])
        half_pi = sb("half_pi", [P, 1])
        tiny = sb("tiny", [P, 1])
        b_mag_half = sb("b_mag_half", [P, 1])
        minus_half = sb("minus_half", [P, NT])
        euler = sb("euler", [P, NT * E1])
        phi, cos_phi, sin_phi = sb("phi", [P, S]), sb("cos_phi", [P, S]), sb("sin_phi", [P, S])
        w1g = sb("w1g", [P, CTX, G1 + 1])
        b1_all, b2_all = sb("b1_all", [P, G1]), sb("b2_all", [P, D])

        x_next, xin = sb("x_next", [P, NT, D]), sb("xin", [P, NT, D])
        z = sb("z", [P, NT, D])
        zs = sb("zs", [P, NT, D])
        bn6, mv, rstd = sb("bn6", [P, NT, 6]), sb("mv", [P, NT, 2]), sb("rstd", [P, NT])
        bn6_n, mv_n, rstd_n = sb("bn6_n", [P, NT, 6]), sb("mv_n", [P, NT, 2]), sb("rstd_n", [P, NT])
        ssq = sb("ssq", [P, NT])
        xT = sb("xT", [P, S])
        nT = sb("nT", [P, S])
        x_hi, x_lo = sb("x_hi", [P, S], F32R), sb("x_lo", [P, S], F32R)
        parts = sb("parts", [P, 2, PIECES, S], BF16)
        rest = sb("rest", [P, 2, S])
        q_st, k_st = sb("q_st", [P, 2, HJ, S], BF16), sb("k_st", [P, HJ, S], BF16)
        v_aug = sb("v_aug", [P, NT * H, 32])
        hid = sb("hid", [P, C0, S])
        part_y = sb("part_y", [P, 2, NT, D])
        smax = sb("smax", [P, NT, H])
        mrest = sb("mrest", [P, NT, HJ])
        mp = sb("mp", [P, NT, PIECES * HJ], BF16)
        mpt = sb("mpt", [PIECES * HJ, S], BF16)
        probs = sb("probs", [P, 2, 4, S])
        o_sb = sb("o_sb", [P, S])
        oden = sb("oden", [P, NT * 4, 1])
        on = sb("on", [P, NT, 4, 32])
        hT = sb("hT", [P, S])
        gate = sb("gate", [P, NT, D])
        x1 = sb("x1", [P, NT, D])
        outb = sb("outb", [P, NT, D])
        lg = sb("lg", [P, NT, 12])
        lm = sb("lm", [P, NT, 5])
        le = sb("le", [P, NT, 12])
        ld = sb("ld", [P, NT, 12])
        lt = sb("lt", [P, NT, 12])
        beat, tie = sb("beat", [P, NT * 8 * 8]), sb("tie", [P, NT * 8 * 8])
        rank = sb("rank", [P, NT * 8])
        cw = sb("cw", [P, NT, E0])
        wsum = sb("wsum", [P, NT])
        gw, first_wins = sb("gw", [P, NT, GROUPS]), sb("first_wins", [P, NT, GROUPS])
        tg, wgt, turns, phq = (probs[:, 0, n, :] for n in range(4))
        ph_abs, cq, sq, wc = (probs[:, 1, n, :] for n in range(4))
        ga = probs[:, 0, 0:2, :].rearrange("p a (t g) -> p (a t) g", t=2)
        gT = probs[:, 0, 2:4, :]
        mem = sb("mem", [P, 2, S])
        mem_r, mem_i = mem[:, 0, :], mem[:, 1, :]
        ctxt, squares = hid[:, 8:12, :], hid[:, 12:15, :]
        ws, acc, inv = sb("ws", [P, S]), sb("acc", [P, S]), sb("inv", [P, S])
        stat = sb("stat", [P, NT, 2])
        var = sb("var", [P, NT])
        yn = sb("yn", [P, NT, D])

        scr = [nc.dram_tensor(f"scr_{n}", [PIECES, 2, HD * HJ, S], BF16).ap() for n in "qk"]
        scr_m = nc.dram_tensor("scr_m", [2, PIECES * HJ, S], BF16).ap()
        zeros = nc.dram_tensor("zeros", [PIECES, HJ, S], BF16).ap()

        ps_s = psum("ps_s", [P, 4, S])
        ps_u = psum("ps_u", [P, 2, S])
        ps_y = psum("ps_y", [P, S])
        ps_m = psum("ps_m", [P, S])
        ps_u16 = ps_u[:, 0, :].bitcast(BF16)
        y_bank = (ps_y, ps_m)

        def y2_bank(ex):
            return (ps_y[:, :], ps_m[:, :], ps_u[:, 0, :], ps_u[:, 1, :])[ex % 4 if ex < 7 else 0]

        def u_bank(loop, c):
            if loop == 0 and c < 3:
                return ps_s[:, (0, 1, 3)[c], :]
            ring = (ps_u[:, 0, :], ps_u[:, 1, :], ps_y[:, :])
            return ring[c % 3] if c < 12 else ring[c % 2]

        def last_bank(t):
            return ps_m if t < NT // 2 else ps_u[:, 1, :]


        def sem(name):
            return ctx.enter_context(nc.semaphore(name))

        first_in, second_in, v_in = sem("first_in"), sem("second_in"), sem("v_in")
        w_in = sem("w_in")
        x_in, stored, zeroed = sem("x_in"), sem("stored"), sem("zeroed")
        set_up = sem("set_up")
        set_pool, set_pe, set_act = sem("set_pool"), sem("set_pe"), sem("set_act")
        met = sem("met")
        split_set = sem("weights_split")
        go = {n: sem(f"go_{n}") for n in ("pe", "act", "dve", "pool")}

        body = {}

        for name in (
            "nstats_ok nrstd_ok nz_ok nssq_ok nzs_ok nzT_ps nT_ok qkv_ps part_ok rest_ok parts_ok v_ok "
            "scr_out stack_in x_used ssq_ok rstd_ok zs_ok z_ok zT_ps xT_ok hi_ok lo_ok lg_ps lg_ok lt_in lt_ok "
            "cw_ok u_ps h_ok y_ps yc_ok za_ok zc_ok s1_ps max_ok mp_ok mpt_ps mpt_ok m_out early_shift late_shift s2_ps p_ok "
            "pv_ps o_ok oN_ps on_ok onT_ps hT_ok att_ps gate_ok x1_ok stats_ok yn_ok ynb_ok mq_ps r_ok b_ok abs_ok head_T_ps head_xT_ok head_hi_ok head_lo_ok head_lg_ps head_u_ps tg_ok ph_ok "
            "sc_ok acc_ok inv_in mem_ok f_ps a_ok sg_in sg_ok c01_ok rot_in ri_ok sq_ok g_ps var_ok ga_ok "
            "ge_ok gT_ps gT_ok mlp_ps share_ok out_ok dve pool"
        ).split():
            body[name] = sem(name)
        numbers = sorted(int(s.num) for s in body.values())
        assert numbers[-1] - numbers[0] == len(numbers) - 1
        w = type("W", (), body)
        shifted = (w.early_shift, w.late_shift)

        DVE_SHARES = 3
        ACT_SHARES = 4
        HEAD_CHUNKS = 4
        POOL_SQUARES = range(0, 6)
        UNITS = 2 * H
        ROUND_UNITS = UNITS // 2
        ORDER = [half * HJ + 2 * g + a for g in range(4) for half in range(2) for a in range(2)]
        after = {}
        for n in range(UNITS):
            r_ = n % ROUND_UNITS
            if n < ROUND_UNITS:
                at = (0, (5, 6, 7, 9)[r_] if r_ < 4 else 10 + r_)
            else:
                at = (1, (-1, -1, 3, 6, 8)[r_] if r_ < 5 else 7 + r_)
            after.setdefault(at, []).append(n)

        block = ctx.enter_context(nc.Block())

        @block.sync
        def _(e):
            def stack(in_body):
                for which in range(2):
                    e.wait_ge(w.parts_ok, which + 1)
                    e.dma_start(scr[which].rearrange("a h r n -> (h r) a n"), parts[:, which, :, :]
                                ).then_inc(w.scr_out, 16)
                if in_body:
                    e.wait_ge(w.s2_ps, 2 * 4 * NT)
                e.wait_ge(w.scr_out, 32)
                for which in range(2):
                    for half in range(2):
                        dst = k_st if which else q_st[:, half]
                        for pattern in (STACK_K if which else STACK_Q):
                            row, first_part, step, n = pattern
                            src = scr[which][first_part:first_part + 1 + step * (n - 1), half]
                            src = src.rearrange("c (k j) n -> k c (j n)", j=HJ)
                            if n > 1 and step == 0:
                                src = src.to_broadcast([HD, n, HJ * S])
                            at = 64 * half + row
                            e.dma_start(dst[at:at + HD * n, :, :].rearrange("r j n -> r (j n)"), src
                                        ).then_inc(w.stack_in, 16)
                for half in range(2):
                    e.dma_start(q_st[64 * half + ROWS:64 * half + ROWS + PIECES, half], zeros
                                ).then_inc(w.stack_in, 16)

            def shift(r):
                e.wait_ge(w.mpt_ok, r + 1)
                e.dma_start(scr_m[r], mpt[:, :]).then_inc(w.m_out, 16)
                e.wait_ge(w.m_out, 16 * (r + 1))
                src = scr_m[r].rearrange("(p g h a) n -> p g h a n", g=2, h=2, a=2)
                for half in range(2):
                    at = 64 * half + ROWS
                    for g in range(2):
                        e.dma_start(q_st[at:at + PIECES, half, 4 * r + 2 * g:4 * r + 2 * g + 2, :], src[:, g, half]
                                    ).then_inc(shifted[r], 16)

            def gather():
                e.wait_ge(met, 4)
                e.nop().then_inc(met, -4)
                e.sem_clear(range(numbers[0], numbers[-1] + 1))
                for n in go:
                    e.sem_inc(go[n], 1)

            e.dma_start(x_next[:, :, :], x[0:1].rearrange("o (t p) d -> p (o t) d", p=P)).then_inc(x_in, 16)
            e.dma_start(c_first[:, :], first).then_inc(first_in, 16)
            e.dma_start(hid[:, 0:4, :], w1.rearrange("p (a n) -> p a n", a=4)).then_inc(w_in, 16)
            e.dma_start(c_second[:, :], second).then_inc(second_in, 16)
            e.dma_start(rows_sb[:, :], rows).then_inc(second_in, 16)
            e.dma_start(hid[:, 4:6, :], v1.rearrange("p (a n) -> p a n", a=2)).then_inc(w_in, 16)
            e.wait_ge(set_pool, 1)
            e.dma_start(zeros, q_st[64:64 + PIECES, 0]).then_inc(zeroed, 16)
            e.wait_ge(zeroed, 16)
            stack(False)
            e.dma_start(w2_sb[:, :, :], w2.rearrange("p (c d) -> p c d", c=C0)).then_inc(v_in, 16)
            e.dma_start(v2_sb[:, :, :], v2.rearrange("p (c d) -> p c d", c=E1)).then_inc(v_in, 16)
            e.wait_ge(w.stack_in, 16 * STACK_DMAS)
            e.sem_inc(stored, 16)
            gather()
            with e.Fori(0, B) as b:
                e.wait_ge(w.x_used, 1)
                e.dma_start(x_next[:, :, :], x[bass.ds((b + 1) & (B - 1), 1)].rearrange("o (t p) d -> p (o t) d", p=P)
                            ).then_inc(x_in, 16)
                shift(0)
                shift(1)
                stack(True)
                e.wait_ge(w.out_ok, 1)
                e.dma_start(out[bass.ds(b, 1)].rearrange("o (t p) d -> p (o t) d", p=P), outb[:, :, :]
                            ).then_inc(stored, 16)
                e.wait_ge(w.stack_in, 16 * STACK_DMAS)
                gather()
            e.wait_ge(stored, 16)

        def meet(e, name):
            e.drain().then_inc(met, 1)
            e.wait_ge(go[name], 1)
            e.nop().then_inc(go[name], -1)

        @block.tensor
        def _(e):
            def transposed(src, dst, idt, done):
                for t in range(NT):
                    i = e.transpose(dst(t), src(t), idt)
                i.then_inc(done, 1)

            def next_T(in_body):
                e.wait_ge(w.nz_ok, 1)
                if in_body:
                    e.wait_ge(w.p_ok, 2 * 4 * NT)
                transposed(lambda t: z[:, t, :], lambda t: ps_s[:, 3, t * P:(t + 1) * P], ident, w.nzT_ps)

            def next_q():
                e.wait_ge(w.nT_ok, 1)
                e.matmul(ps_s[:, 0, :], wq, nT[:, :], start=True, stop=True).then_inc(w.qkv_ps, 1)

            def next_k():
                e.matmul(ps_s[:, 1, :], wk, nT[:, :], start=True, stop=True).then_inc(w.qkv_ps, 1)

            def next_v():
                for t in range(NT):
                    i = e.matmul(ps_s[:, 2, t * P:(t + 1) * P], nT[:, t * P:(t + 1) * P], wv, start=True, stop=True)
                i.then_inc(w.qkv_ps, 1)

            def keep_busy(bank, n):
                for _ in range(n):
                    e.matmul(bank, w1_hi[:, 0:P], w1_hi[:, 0:S], start=True, stop=True)

            def unit(n):
                if n >= 2:
                    e.wait_ge(w.max_ok, n - 1)
                elif n:
                    e.wait_ge(w.lg_ok, 1)
                    e.wait_ge(w.h_ok, 3)
                else:
                    e.wait_ge(w.h_ok, 2)
                half, j = ORDER[n // 2] // HJ, ORDER[n // 2] % HJ
                for a in range(2):
                    t = 2 * (n % 2) + a
                    i = e.matmul(ps_s[:, t, :], q_st[:, half, j, t * P:(t + 1) * P], k_st[:, j, :],
                                 start=True, stop=True)
                i.then_inc(w.s1_ps, 1)

            def shift_rows(r):
                e.wait_ge(w.mp_ok, r + 1)
                e.wait_ge(w.h_ok, C0 * (r + 1))
                transposed(lambda t: mp[:, t, :], lambda t: ps_u16[0:PIECES * HJ, t * P:(t + 1) * P],
                           ident_b[:, :], w.mpt_ps)

            def logits(bank, done):
                for t in range(NT):
                    i = e.matmul(bank[:, t * 12:(t + 1) * 12], xT[:, t * P:(t + 1) * P], wr, start=True, stop=True)
                i.then_inc(done, 1)

            def first_chunk(u, c, low_ready, done):
                cols = slice(c * P, (c + 1) * P)
                e.matmul(u, w1_hi[:, cols], x_hi[:, :], start=True, stop=False)
                e.matmul(u, w1_lo[:, cols], x_hi[:, :], start=False, stop=False)
                if low_ready is not None:
                    e.wait_ge(low_ready, 1)
                e.matmul(u, w1_hi[:, cols], x_lo[:, :], start=False, stop=True).then_inc(done, 1)

            def head_T():
                e.wait_ge(w.nzs_ok, 1)
                transposed(lambda t: zs[:, t, :], lambda t: ps_s[:, 3, t * P:(t + 1) * P], ident, w.head_T_ps)

            def head_logits():
                e.wait_ge(w.head_xT_ok, 1)
                logits(ps_s[:, 2, :], w.head_lg_ps)

            def head_chunks():
                e.wait_ge(w.head_hi_ok, 1)
                for c in range(HEAD_CHUNKS):
                    first_chunk(u_bank(0, c), c, w.head_lo_ok if c == 0 else None, w.head_u_ps)

            def second_product(bank, n, ex, t, weights, per):
                for c in range(per):
                    m = per * ex + c
                    i = e.matmul(bank[:, t * P:(t + 1) * P], hid[:, m, t * P:(t + 1) * P], weights[:, m, :],
                                 start=c == 0, stop=c == per - 1)
                if t == NT - 1 or (n < LOOPS and ex == E0 - 1 and t == NT // 2 - 1):
                    i.then_inc(w.y_ps, 1)

            e.wait_ge(first_in, 16)
            next_T(False)
            next_q()
            next_k()
            next_v()
            e.wait_ge(split_set, 1)
            head_T()
            head_logits()
            head_chunks()
            e.wait_ge(set_pe, 1)
            for c in range(CTX):
                i = e.matmul(ps_y[:, 0:G1], ones[:, :], w1g[:, c, 0:G1], start=c == 0, stop=c == CTX - 1)
            for c in range(CTX):
                e.matmul(ps_m[:, 0:G1], hid[:, 8, c * P:(c + 1) * P], w1m[:, c, :], start=c == 0, stop=False)
            e.matmul(ps_m[:, 0:G1], ones[0:1, :], rows_sb[:, 0:G1], start=False, stop=True)
            i = e.matmul(ps_m[:, G1:G1 + D], ones[0:1, :], rows_sb[:, G1:G1 + D], start=True, stop=True)
            i.then_inc(set_act, 1)
            e.wait_ge(v_in, 32)
            meet(e, "pe")

            with e.Fori(0, B):
                for loop in range(LOOPS):
                    if loop:
                        for m in after[(1, -1)]:
                            unit(m)
                        e.wait_ge(w.mpt_ok, 1)
                        keep_busy(ps_u[:, 0, :], 12)
                        for t in range(NT):
                            e.wait_ge(w.zs_ok, t + 1)
                            i = e.transpose(ps_m[:, t * P:(t + 1) * P], zs[:, t, :], ident)
                        i.then_inc(w.zT_ps, 1)
                        e.wait_ge(w.xT_ok, 1)
                        logits(ps_m, w.lg_ps)
                        e.wait_ge(w.hi_ok, 1)
                        e.wait_ge(w.mpt_ok, 1)
                    for i_ in range(0 if loop else HEAD_CHUNKS, C0):
                        n = C0 * loop + i_
                        if loop or i_ >= 6:
                            if i_ >= 3:
                                e.wait_ge(w.h_ok, n - 2 if i_ < 14 else n - 1)
                        first_chunk(u_bank(loop, i_), i_, w.lo_ok if n == C0 else None, w.u_ps)
                        for m in after.get((loop, i_), ()):
                            unit(m)
                    for ex in range(E0):
                        e.wait_ge(w.h_ok, C0 * loop + 2 * ex + 2)
                        if ex == 1 and loop:
                            e.wait_ge(w.lg_ok, 2)
                        if 2 <= ex < E0 - DVE_SHARES + 2:
                            e.wait_ge(w.yc_ok, (E0 - DVE_SHARES) * loop + ex - 1)
                        elif ex >= 2:
                            e.wait_ge(w.z_ok, NT * (DVE_SHARES * loop + ex - 1 - E0 + DVE_SHARES))
                        if ex == E0 - 1:
                            shift_rows(loop)
                        for t in range(NT):
                            bank = last_bank(t) if ex == E0 - 1 else y_bank[ex % 2]
                            second_product(bank, loop, ex, t, w2_sb, 2)
                            if t % 2:
                                for m in after.get((loop, C0 + 2 * ex + t // 2), ()):
                                    unit(m)

                def heads(g):
                    return [(0, 2 * g), (0, 2 * g + 1), (1, 2 * g), (1, 2 * g + 1)]

                def scores(v, pair):
                    g, kt = v // NT, v % NT
                    if v == 0:
                        e.wait_ge(w.max_ok, UNITS - 1 + pair)
                        e.wait_ge(w.early_shift, 64)
                    else:
                        e.wait_ge(w.p_ok, 2 * (v - 1) + pair + 1)
                    if g == 2 and kt == 0:
                        e.wait_ge(w.late_shift, 64)
                    for a in range(2):
                        half, j = heads(g)[2 * pair + a]
                        i = e.matmul(ps_s[:, 2 * pair + a, :], k_st[:, j, kt * P:(kt + 1) * P], q_st[:, half, j, :],
                                     start=True, stop=True)
                    i.then_inc(w.s2_ps, 1)

                def values(v):
                    g, kt = v // NT, v % NT
                    e.wait_ge(w.p_ok, 2 * v + 2)
                    if kt == 0:
                        if g >= 2:
                            e.wait_ge(w.o_ok, g - 1)
                        elif g == 1:
                            e.wait_ge(w.z_ok, DVE_SHARES * NT * LOOPS)
                        else:
                            e.wait_ge(w.mpt_ok, 2)
                    for a, (half, j) in enumerate(heads(g)):
                        i = e.matmul(ps_u[32 * a:32 * a + 32, g % 2, :], v_aug[:, kt * H + HJ * half + j, :],
                                     probs[:, v % 2, a, :], start=kt == 0, stop=kt == NT - 1,
                                     tile_position=(0, 32 * a))
                    i.then_inc(w.pv_ps, 1)

                def back(g):
                    e.wait_ge(w.o_ok, g + 1)
                    if g:
                        e.wait_ge(w.on_ok, g)
                    else:
                        e.wait_ge(w.z_ok, DVE_SHARES * NT * LOOPS)
                    transposed(lambda t: o_sb[:, t * P:(t + 1) * P], lambda t: ps_m[:, t * P:(t + 1) * P],
                               ident, w.oN_ps)

                scores(0, 0)
                scores(0, 1)
                for v in range(4 * NT):
                    if v + 1 < 4 * NT:
                        scores(v + 1, 0)
                        scores(v + 1, 1)
                    values(v)
                    if v % NT == 1 and v > NT:
                        back(v // NT - 1)
                next_T(True)
                back(3)
                next_q()
                e.wait_ge(w.on_ok, 4)
                transposed(lambda t: on[:, t, :, :].rearrange("p g k -> p (g k)"),
                           lambda t: ps_m[:, t * P:(t + 1) * P], ident, w.onT_ps)
                e.wait_ge(w.hT_ok, 1)
                for t in range(NT):
                    i = e.matmul(ps_y[:, t * P:(t + 1) * P], hT[:, t * P:(t + 1) * P], wo, start=True, stop=True)
                i.then_inc(w.att_ps, 1)
                next_k()
                next_v()
                keep_busy(ps_s[:, 3, :], 12)

                for t in range(NT):
                    e.wait_ge(w.yn_ok, t + 1)
                    i = e.transpose(ps_m[:, t * P:(t + 1) * P], yn[:, t, :], ident)
                i.then_inc(w.zT_ps, 1)
                e.wait_ge(w.xT_ok, LOOPS)
                e.wait_ge(w.o_ok, 4)
                e.matmul(ps_u[:, 0, :], w_mag, xT[:, :], start=True, stop=True).then_inc(w.mq_ps, 1)
                for t in range(NT):
                    i = e.matmul(ps_m[:, t * E1:(t + 1) * E1], xT[:, t * P:(t + 1) * P], wr1,
                                 start=True, stop=True)
                i.then_inc(w.lg_ps, 1)
                e.matmul(ps_u[:, 1, :], w_q, xT[:, :], start=True, stop=True).then_inc(w.mq_ps, 1)
                e.wait_ge(w.hi_ok, LOOPS)
                e.wait_ge(w.rest_ok, 2)
                e.wait_ge(w.part_ok, 2)
                for i_ in range(E1):
                    if i_ == 2:
                        e.wait_ge(w.v_ok, 1)
                    if i_ >= 4:
                        e.wait_ge(w.r_ok, i_ - 3)
                    u, cols = ps_s[:, i_ % 4, :], slice(i_ * P, (i_ + 1) * P)
                    e.matmul(u, v1_hi[:, cols], x_hi[:, :], start=True, stop=False)
                    e.matmul(u, v1_lo[:, cols], x_hi[:, :], start=False, stop=False)
                    if i_ == 0:
                        e.wait_ge(w.lo_ok, LOOPS)
                    e.matmul(u, v1_hi[:, cols], x_lo[:, :], start=False, stop=True).then_inc(w.f_ps, 1)

                def second_of(ex):
                    if ex in POOL_SQUARES:
                        e.wait_ge(w.b_ok, ex + 1)
                    else:
                        e.wait_ge(w.a_ok, ex + 1 - len(POOL_SQUARES))
                    if ex < 4:
                        e.wait_ge((w.x1_ok, w.sg_in, w.tg_ok, w.ph_ok)[ex], 1)
                    elif ex < 7:
                        e.wait_ge(w.yc_ok, (E0 - DVE_SHARES) * LOOPS + ex - 3)
                    else:
                        e.wait_ge(w.share_ok, 1)
                    for t in range(NT):
                        second_product(y2_bank(ex), LOOPS, ex, t, v2_sb, 1)

                e.wait_ge(w.r_ok, E1)
                e.wait_ge(w.c01_ok, 2)
                for t in range(NT):
                    for c in range(2):
                        e.matmul(ps_s[:, t, 0:G1 + 1], ctxt[:, c, t * P:(t + 1) * P], w1g[:, c, :],
                                 start=c == 0, stop=False)
                for ex in range(4):
                    second_of(ex)
                e.wait_ge(w.sq_ok, 3)
                for t in range(NT):
                    for c in range(3):
                        e.matmul(ps_s[:, t, G1 + 1:G1 + 2], squares[:, c, t * P:(t + 1) * P],
                                 mean_col[:, :], start=False, stop=False)
                e.wait_ge(w.ri_ok, 2)
                for t in range(NT):
                    for c in range(2, CTX):
                        i = e.matmul(ps_s[:, t, 0:G1 + 1], ctxt[:, c, t * P:(t + 1) * P], w1g[:, c, :],
                                     start=False, stop=c == CTX - 1)
                i.then_inc(w.g_ps, 1)
                second_of(4)
                second_of(5)
                for t in range(NT):
                    e.wait_ge(w.ge_ok, t + 1)
                    if t == 0:
                        e.wait_ge(w.ga_ok, NT)
                    for c in range(2):
                        i = e.transpose(ps_s[:, c, t * P:(t + 1) * P], ga[:, t, c * P:(c + 1) * P], ident)
                i.then_inc(w.gT_ps, 1)
                head_T()
                second_of(6)
                head_logits()
                second_of(7)
                e.wait_ge(w.gT_ok, 1)
                e.wait_ge(w.yc_ok, (E0 - DVE_SHARES) * LOOPS + 4)
                for t in range(NT):
                    for c in range(2):
                        i = e.matmul(ps_u[:, 1, t * P:(t + 1) * P], gT[:, c, t * P:(t + 1) * P], w2m[:, c, :],
                                     start=c == 0, stop=c == 1)
                i.then_inc(w.mlp_ps, 1)
                e.wait_ge(w.share_ok, 3)
                head_chunks()
                meet(e, "pe")

        @block.scalar
        def _(e):
            a = e.activation

            def next_T():
                e.wait_ge(w.nzT_ps, 1)
                e.copy(nT[:, :], ps_s[:, 3, :]).then_inc(w.nT_ok, 1)

            def next_first():
                for which in range(2):
                    e.wait_ge(w.qkv_ps, which + 1)
                    e.copy(parts[:, which, 0, :], ps_s[:, which, :]).then_inc(w.part_ok, 1)

            def next_second():
                for which in range(2):
                    e.wait_ge(w.rest_ok, which + 1)
                    e.copy(parts[:, which, 1, :], rest[:, which, :]).then_inc(w.part_ok, 1)

            def head_xT():
                e.wait_ge(w.head_T_ps, 1)
                a(xT[:, :], ps_s[:, 3, :], ACT.Copy, scale=f_("norm_w")).then_inc(w.head_xT_ok, 1)

            def weighted(n, ex, dst, bank):
                e.wait_ge(w.y_ps, (E0 + 1) * n + ex + 1)
                for t in range(NT):
                    i = a(dst[:, t, :], bank[:, t * P:(t + 1) * P], ACT.Copy, scale=cw[:, t, ex:ex + 1])
                i.then_inc(w.yc_ok, 1)

            next_T()
            next_first()
            next_second()
            e.wait_ge(set_up, 8)
            head_xT()
            a(sin_phi[:, :], ws[:, :], ACT.Sin)
            a(cos_phi[:, :], ph_abs, ACT.Sin, bias=half_pi[:, :], scale=-1.0)
            e.wait_ge(set_act, 1)
            e.copy(b1_all[:, :], ps_m[:, 0:G1])
            e.copy(b2_all[:, :], ps_m[:, G1:G1 + D])
            a(o_sb[:, 0:1], tiny[:, :], ACT.Silu)
            meet(e, "act")

            with e.Fori(0, B):
                for loop in range(LOOPS):
                    if loop:
                        e.wait_ge(w.zT_ps, 1)
                        a(xT[:, :], ps_m[:, :], ACT.Copy, scale=f_("norm_w")).then_inc(w.xT_ok, 1)
                    for i in range(C0):
                        if i == 4:
                            e.wait_ge(w.lt_in, loop + 1)
                            a(lt[:, :, :], ld[:, :, :], ACT.Tanh, scale=0.5).then_inc(w.lt_ok, 1)
                        if loop or i >= HEAD_CHUNKS:
                            e.wait_ge(w.u_ps, C0 * loop + i + 1 - HEAD_CHUNKS)
                        a(hid[:, i, :], u_bank(loop, i), ACT.Silu).then_inc(w.h_ok, 1)
                    e.wait_ge(w.cw_ok, loop + 1)
                    for ex in range(E0 - DVE_SHARES):
                        n = (E0 - DVE_SHARES) * loop + ex
                        if n >= 2:
                            e.wait_ge(w.za_ok, n - 1)
                        weighted(loop, ex, part_y[:, n % 2], y_bank[ex % 2])
                    e.wait_ge(w.mpt_ps, loop + 1)
                    if loop:
                        e.wait_ge(w.m_out, 16)
                    e.copy(mpt[:, :], ps_u16[0:PIECES * HJ, 0:S]).then_inc(w.mpt_ok, 1)
                for v in range(4 * NT):
                    if v >= 2:
                        e.wait_ge(w.pv_ps, v - 1)
                    for pair in range(2):
                        e.wait_ge(w.s2_ps, 2 * v + pair + 1)
                        a(probs[:, v % 2, 2 * pair:2 * pair + 2, :], ps_s[:, 2 * pair:2 * pair + 2, :], ACT.Exp,
                          scale=float(HD) ** -0.5).then_inc(w.p_ok, 1)
                next_T()
                e.wait_ge(w.onT_ps, 1)
                e.copy(hT[:, :], ps_m[:, :]).then_inc(w.hT_ok, 1)
                e.wait_ge(w.zc_ok, 1)
                a(gate[:, :, :], gate[:, :, :], ACT.Silu).then_inc(w.gate_ok, 1)
                next_first()
                e.wait_ge(w.zT_ps, LOOPS)
                e.copy(xT[:, :], ps_m[:, :]).then_inc(w.xT_ok, 1)
                next_second()
                e.wait_ge(w.mq_ps, 1)
                a(tg, ps_u[:, 0, :], ACT.Tanh, bias=b_mag_half[:, :], scale=0.5).then_inc(w.tg_ok, 1)

                def relu(i):
                    e.wait_ge(w.f_ps, i + 1)
                    a(hid[:, i, :], ps_s[:, i % 4, :], ACT.Relu).then_inc(w.r_ok, 1)

                e.wait_ge(w.acc_ok, 1)
                a(acc[:, :], acc[:, :], ACT.Sqrt, bias=tiny[:, :], scale=MAG).then_inc(w.inv_in, 1)
                for i in range(E1):
                    relu(i)
                e.wait_ge(w.ph_ok, 2)
                a(ph_abs, phq, ACT.Abs).then_inc(w.abs_ok, 1)
                a(sq, phq, ACT.Sin).then_inc(w.sc_ok, 1)
                e.wait_ge(w.abs_ok, 1)
                a(cq, ph_abs, ACT.Sin, bias=half_pi[:, :], scale=-1.0).then_inc(w.sc_ok, 1)
                a(squares[:, 2, :], xT[:, :], ACT.Square).then_inc(w.sq_ok, 1)
                for c in range(2):
                    e.wait_ge(w.mem_ok, c + 1)
                    a(squares[:, c, :], mem[:, c, :], ACT.Square).then_inc(w.sq_ok, 1)
                e.wait_ge(w.cw_ok, LOOPS + 1)
                e.wait_ge(w.x1_ok, 1)
                base = (E0 - DVE_SHARES) * LOOPS
                for ex in range(ACT_SHARES):
                    n = base + ex
                    if ex:
                        e.wait_ge(w.za_ok, base + max(ex - 2, 0))
                    weighted(LOOPS, ex, part_y[:, n % 2] if ex else gate, y2_bank(ex))
                for t in range(NT):
                    e.wait_ge(w.ga_ok, t + 1)
                    a(ga[:, t, :], ga[:, t, :], ACT.Gelu).then_inc(w.ge_ok, 1)
                e.wait_ge(w.gT_ps, 1)
                e.copy(gT[:, :, :], ps_s[:, 0:2, :]).then_inc(w.gT_ok, 1)
                e.wait_ge(w.c01_ok, 2)
                head_xT()
                e.wait_ge(w.share_ok, E1 - ACT_SHARES)
                a(gate[:, :, :], gate[:, :, :], ACT.Silu).then_inc(w.gate_ok, 1)
                meet(e, "act")

        @block.gpsimd
        def _(e):
            count = [0]

            def link(ins):
                count[0] += 1
                ins.then_inc(w.pool, 1)
                e.wait_ge(w.pool, count[0])

            def power(dst, src, scale, eps, done):
                link(e.tensor_scalar(dst, src, scale, eps, ALU.mult, ALU.add))
                e.tensor_tensor(dst, dst, minus_half[:, :], ALU.pow).then_inc(done, 1)

            def next_norms():
                e.wait_ge(w.nstats_ok, 1)
                power(rstd_n[:, :], mv_n[:, :, 1], 1.0, 1e-5, w.nrstd_ok)
                e.wait_ge(w.nssq_ok, 1)
                power(rstd_n[:, :], ssq[:, :], 1.0 / D, 1e-6, w.nrstd_ok)

            e.memset(q_st[:, :, :, :], 0.0).then_inc(set_pool, 1)
            e.wait_ge(set_up, 1)
            next_norms()
            meet(e, "pool")
            with e.Fori(0, B):
                count[0] = 0
                e.tensor_copy(xin[:, :, :], x_next[:, :, :]).then_inc(w.x_used, 1)

                def accumulate(n, ex, dst, last_in):
                    e.wait_ge(w.yc_ok, n + 1)
                    link_in = e.tensor_tensor(dst[:, :, :], dst[:, :, :], part_y[:, n % 2], ALU.add)
                    link_in.then_inc(w.za_ok, 1)

                for loop in range(LOOPS):
                    if loop:
                        e.wait_ge(w.ssq_ok, 1)
                        power(rstd[:, :], ssq[:, :], 1.0 / D, 1e-6, w.rstd_ok)
                        e.wait_ge(w.zs_ok, NT)
                    for ex in range(E0 - DVE_SHARES):
                        n = (E0 - DVE_SHARES) * loop + ex
                        if ex:
                            e.wait_ge(w.za_ok, n)
                        accumulate(n, ex, z, n)
                e.wait_ge(w.z_ok, DVE_SHARES * NT * LOOPS)
                e.tensor_copy(gate[:, :, :], z[:, :, :]).then_inc(w.zc_ok, 1)
                next_norms()
                e.wait_ge(w.stats_ok, 1)
                power(rstd[:, :], mv[:, :, 1], 1.0, 1e-5, w.rstd_ok)
                e.wait_ge(w.xT_ok, LOOPS)
                e.tensor_tensor(ctxt[:, 0, :], xT[:, :], cos_phi[:, :], ALU.mult).then_inc(w.c01_ok, 1)
                e.wait_ge(w.sg_in, 1)
                e.tensor_tensor(le[:, :, 0:E1], euler[:, :].rearrange("p (t x) -> p t x", t=NT),
                                ld[:, :, 0:E1], ALU.pow).then_inc(w.sg_ok, 1)
                e.tensor_tensor(ctxt[:, 1, :], xT[:, :], sin_phi[:, :], ALU.mult).then_inc(w.c01_ok, 1)
                for i in POOL_SQUARES[:4]:
                    e.wait_ge(w.r_ok, i + 1)
                    e.tensor_tensor(hid[:, i, :], hid[:, i, :], hid[:, i, :], ALU.mult).then_inc(w.b_ok, 1)
                e.wait_ge(w.mem_ok, 1)
                e.wait_ge(w.sc_ok, 2)
                e.tensor_tensor(wc, mem_r, cq, ALU.mult).then_inc(w.rot_in, 1)
                e.tensor_tensor(ws[:, :], mem_r, sq, ALU.mult).then_inc(w.rot_in, 1)
                for which in range(2):
                    e.wait_ge(w.part_ok, which + 3)
                    e.tensor_tensor(parts[:, which, 2, :], rest[:, which, :], parts[:, which, 1, :], ALU.subtract
                                    ).then_inc(w.parts_ok, 1)
                e.tensor_tensor(yn[:, :, :], yn[:, :, :], b2_all[:, :].unsqueeze(1).to_broadcast([P, NT, D]), ALU.add
                                ).then_inc(w.ynb_ok, 1)
                for i in POOL_SQUARES[4:]:
                    e.wait_ge(w.r_ok, i + 1)
                    e.tensor_tensor(hid[:, i, :], hid[:, i, :], hid[:, i, :], ALU.mult).then_inc(w.b_ok, 1)
                base = (E0 - DVE_SHARES) * LOOPS
                for ex in range(1, ACT_SHARES):
                    n = base + ex
                    if ex == 2:
                        e.wait_ge(w.var_ok, 1)
                        power(rstd[:, :], var[:, :], 1.0, 1e-5, w.rstd_ok)
                    e.wait_ge(w.yc_ok, n + 1)
                    if ex > 1:
                        e.wait_ge(w.za_ok, n - 1)
                    e.tensor_tensor(gate[:, :, :], gate[:, :, :], part_y[:, n % 2], ALU.add).then_inc(w.za_ok, 1)
                meet(e, "pool")

        @block.vector
        def _(e):
            setup = [0]

            def step(ins):
                setup[0] += 1
                ins.then_inc(set_up, 1)
                e.wait_ge(set_up, setup[0])

            tt, ts, stt = e.tensor_tensor, e.tensor_scalar, e.scalar_tensor_tensor

            count = [0]

            def link(ins):
                count[0] += 1
                ins.then_inc(w.dve, 1)
                e.wait_ge(w.dve, count[0])

            def reduce_turns(chain, x_, t_):
                chain(ts(t_, x_, float(1 / (2 * np.pi)), ROUND, ALU.mult, ALU.add))
                chain(ts(t_, t_, ROUND, None, ALU.subtract))
                chain(stt(x_, t_, -TWO_PI_A, x_, ALU.mult, ALU.add))
                chain(stt(x_, t_, -TWO_PI_B, x_, ALU.mult, ALU.add))

            def norm_stats(src, bn, m, done):
                for t in range(NT):
                    i = e.bn_stats(bn[:, t, :], src[:, t, :])
                link(i)
                for t in range(NT):
                    i = e.bn_aggr(m[:, t, :], bn[:, t, :])
                i.then_inc(done, 1)

            def norm_apply(src, dst, m, r, done):
                for t in range(NT):
                    i = ts(dst[:, t, :], src[:, t, :], m[:, t, 0:1], r[:, t:t + 1], ALU.subtract, ALU.mult)
                i.then_inc(done, 1)

            def sum_squares(done):
                for t in range(NT):
                    i = e.tensor_tensor_reduce(zs[:, t, :], z[:, t, :], z[:, t, :], 1.0, 0.0, ALU.mult,
                                               ALU.add, ssq[:, t:t + 1])
                i.then_inc(done, 1)

            def rms_apply(r, done):
                for t in range(NT):
                    i = ts(zs[:, t, :], z[:, t, :], r[:, t:t + 1], None, ALU.mult)
                i.then_inc(done, 1)

            def next_norms():
                e.wait_ge(x_in, 16)
                e.nop().then_inc(x_in, -16)
                norm_stats(x_next, bn6_n, mv_n, w.nstats_ok)
                e.wait_ge(w.nrstd_ok, 1)
                norm_apply(x_next, z, mv_n, rstd_n, w.nz_ok)
                e.wait_ge(w.nz_ok, 1)
                sum_squares(w.nssq_ok)
                e.wait_ge(w.nrstd_ok, 2)
                rms_apply(rstd_n, w.nzs_ok)

            def split_x(n, ready, hi_ok, lo_ok):
                e.wait_ge(ready, n)
                e.tensor_copy(x_hi[:, :], xT[:, :]).then_inc(hi_ok, 1)
                e.wait_ge(hi_ok, n)
                tt(x_lo[:, :], xT[:, :], x_hi[:, :].bitcast(F32), ALU.subtract).then_inc(lo_ok, 1)

            def next_rest():
                for which in range(2):
                    e.wait_ge(w.part_ok, which + 1)
                    tt(rest[:, which, :], ps_s[:, which, :], parts[:, which, 0, :], ALU.subtract
                       ).then_inc(w.rest_ok, 1)

            def next_third():
                for which in range(2):
                    e.wait_ge(w.part_ok, which + 3)
                    tt(parts[:, which, 2, :], rest[:, which, :], parts[:, which, 1, :], ALU.subtract
                       ).then_inc(w.parts_ok, 1)

            def next_v():
                e.wait_ge(w.qkv_ps, 3)
                e.tensor_copy(v_aug[:, :, 0:HD], ps_s[:, 2, :].rearrange("p (a v) -> p a v", v=HD)
                              ).then_inc(w.v_ok, 1)

            for tile, value in ((minus_half, -0.5), (half_pi, float(np.pi / 2)), (tiny, 1e-8),
                                (euler, float(np.e)), (mean_col, 1.0 / (CTX * P)), (ones, 1.0), (ones_row, 1.0)):
                i = e.memset(tile[:, :], value)
            step(i)
            next_norms()
            e.wait_ge(first_in, 16)
            step(ts(phi[:, :], f_("pos"), f_("phases"), 0.01, ALU.mult, ALU.mult))
            step(e.tensor_copy(ws[:, :], phi[:, :]))
            reduce_turns(step, ws[:, :], wc)
            e.memset(v_aug[:, :, :], 0.0)
            e.memset(k_st[:, :, :], 1.0)
            e.tensor_copy(ident_b[:, :], ident)
            next_rest()
            next_third()
            stt(ph_abs, ws[:, :], -1.0, ws[:, :], ALU.mult, ALU.max)
            step(ts(ws[:, :], ws[:, :], PI_BELOW, -PI_BELOW, ALU.min, ALU.max))
            step(e.memset(v_aug[:, :, HD:HD + 1], 1.0))
            next_v()
            e.wait_ge(w_in, 32)
            wv1 = hid[:, 0:4, :].rearrange("p a n -> p (a n)")
            vv1 = hid[:, 4:6, :].rearrange("p a n -> p (a n)")
            e.tensor_copy(w1_hi[:, :], wv1)
            step(e.tensor_copy(v1_hi[:, :], vv1))
            tt(w1_lo[:, :], wv1, w1_hi[:, :].bitcast(F32), ALU.subtract)
            tt(v1_lo[:, :], vv1, v1_hi[:, :].bitcast(F32), ALU.subtract).then_inc(split_set, 1)
            split_x(1, w.head_xT_ok, w.head_hi_ok, w.head_lo_ok)
            e.wait_ge(second_in, 32)
            for c in range(CTX):
                ts(w1g[:, c, 0:G1], w1m[:, c, :], f_("ln_g")[:, c:c + 1], None, ALU.mult)
                ts(hid[:, 8, c * P:(c + 1) * P], ones[:, :], f_("ln_b")[:, c:c + 1], None, ALU.mult)
                e.memset(w1g[:, c, G1:G1 + 1], 1.0 / (CTX * P))
            e.tensor_scalar(b_mag_half[:, :], f_("b_mag"), 0.5, None, ALU.mult).then_inc(set_pe, 1)
            e.wait_ge(set_act, 1)
            for c in range(CTX):
                i = stt(w1g[:, c, 0:G1], ps_y[:, 0:G1], -1.0 / (CTX * P), w1g[:, c, 0:G1], ALU.mult, ALU.add)
            meet(e, "dve")

            def rank_of(p, n, mask):
                sh = [P, NT, n, n]
                mine = p.unsqueeze(3).to_broadcast(sh)
                theirs = p.unsqueeze(2).to_broadcast(sh)
                b4 = beat[:, 0:NT * n * n].rearrange("p (t i j) -> p t i j", t=NT, i=n)
                t4 = tie[:, 0:NT * n * n].rearrange("p (t i j) -> p t i j", t=NT, i=n)
                tt(b4, theirs, mine, ALU.is_gt)
                link(tt(t4, theirs, mine, ALU.is_equal))
                link(tt(t4, t4, mask, ALU.mult))
                link(tt(b4, b4, t4, ALU.add))
                rk = rank[:, 0:NT * n].rearrange("p (t i) -> p t i", t=NT)
                link(e.tensor_reduce(rk, b4, AX.X, ALU.add))
                return rk

            def bcast(v, n):
                return v.unsqueeze(2).to_broadcast([P, NT, n])

            low4 = lower[:, 0:16].rearrange("p (i j) -> p i j", i=4)
            low8 = lower[:, 64:128].rearrange("p (i j) -> p i j", i=8)

            def router0_a(loop):
                if loop:
                    e.wait_ge(w.lg_ps, 1)
                src = ps_m if loop else ps_s[:, 2, :]
                e.tensor_copy(lg[:, :, :], src[:, 0:NT * 12].rearrange("p (t x) -> p t x", t=NT)
                              ).then_inc(w.lg_ok, 1)
                e.wait_ge(w.lg_ok, loop + 1)
                pair = lg[:, :, 4:12].rearrange("p t (g e) -> p t g e", e=2)
                e.tensor_reduce(lm[:, :, 0:1], lg[:, :, 0:4], AX.X, ALU.max)
                link(e.tensor_reduce(lm[:, :, 1:5], pair, AX.X, ALU.max))
                tt(ld[:, :, 0:4], lg[:, :, 0:4], lm[:, :, 0:1].to_broadcast([P, NT, 4]), ALU.subtract)
                tt(ld[:, :, 4:12].rearrange("p t (g e) -> p t g e", e=2), pair,
                   lm[:, :, 1:5].unsqueeze(3).to_broadcast([P, NT, 4, 2]), ALU.subtract).then_inc(w.lt_in, 1)

            def router0_ranks(loop):
                pair = lg[:, :, 4:12].rearrange("p t (g e) -> p t g e", e=2)
                e.wait_ge(w.lg_ok, loop + 1)
                tt(first_wins[:, :, :], pair[:, :, :, 0], pair[:, :, :, 1], ALU.is_ge)
                rank_of(lg[:, :, 0:4], 4, low4.unsqueeze(1).to_broadcast([P, NT, 4, 4]))

            def router0_b(loop):
                e.wait_ge(w.lt_ok, loop + 1)
                link(ts(ld[:, :, :], lt[:, :, :], -1.0, 1.0, ALU.mult, ALU.add))
                link(e.reciprocal(ld[:, :, :], ld[:, :, :]))
                link(stt(le[:, :, :].rearrange("p t x -> p (t x)"), lt[:, :, :].rearrange("p t x -> p (t x)"), 1.0,
                         ld[:, :, :].rearrange("p t x -> p (t x)"), ALU.add, ALU.mult))
                pair = le[:, :, 4:12].rearrange("p t (g e) -> p t g e", e=2)
                e.tensor_reduce(lm[:, :, 0:1], le[:, :, 0:4], AX.X, ALU.add)
                e.tensor_reduce(lm[:, :, 1:5], pair, AX.X, ALU.add)
                link(stt(gw[:, :, :], rank[:, 0:NT * 4].rearrange("p (t i) -> p t i", t=NT), 1.5, le[:, :, 0:4],
                         ALU.is_lt, ALU.mult))
                link(e.tensor_reduce(wsum[:, :], gw[:, :, :], AX.X, ALU.add))
                ts(lm[:, :, 1:5], lm[:, :, 1:5], 1e-9, 1.0, ALU.mult, ALU.add)
                link(stt(wsum[:, :], lm[:, :, 0], 1e-9, wsum[:, :], ALU.mult, ALU.add))
                link(tt(lm[:, :, 1:5], lm[:, :, 1:5], bcast(wsum[:, :], 4), ALU.mult))
                link(e.reciprocal(lm[:, :, 1:5], lm[:, :, 1:5]))
                link(tt(gw[:, :, :], gw[:, :, :], lm[:, :, 1:5], ALU.mult))
                cwp = cw[:, :, :].rearrange("p t (g e) -> p t g e", e=2)
                link(tt(cwp[:, :, :, 0], first_wins[:, :, :], gw[:, :, :], ALU.mult))
                tt(cwp[:, :, :, 1], gw[:, :, :], cwp[:, :, :, 0], ALU.subtract).then_inc(w.cw_ok, 1)

            def max_of(n):
                e.wait_ge(w.s1_ps, n + 1)
                t = 2 * (n % 2)
                e.tensor_reduce(smax[:, t:t + 2, n // 2], ps_s[:, t:t + 2, :], AX.X, ALU.max).then_inc(w.max_ok, 1)

            def negated_maxima(r):
                e.wait_ge(w.max_ok, ROUND_UNITS * (r + 1))
                if r:
                    e.wait_ge(w.mpt_ps, r)
                sm = smax[:, :, HJ * r:HJ * (r + 1)]
                link(ts(mp[:, :, 0:HJ], sm, -1.0, None, ALU.mult))
                link(stt(mrest[:, :, :], sm, -1.0, mp[:, :, 0:HJ], ALU.mult, ALU.subtract))
                link(e.tensor_copy(mp[:, :, HJ:2 * HJ], mrest[:, :, :]))
                tt(mp[:, :, 2 * HJ:3 * HJ], mrest[:, :, :], mp[:, :, HJ:2 * HJ], ALU.subtract
                   ).then_inc(w.mp_ok, 1)

            with e.Fori(0, B):
                count[0] = 0
                for loop in range(LOOPS):
                    if loop:
                        split_x(1, w.xT_ok, w.hi_ok, w.lo_ok)
                    router0_a(loop)
                    first_unit = ROUND_UNITS * loop + loop
                    max_of(first_unit)
                    router0_ranks(loop)
                    max_of(first_unit + 1)
                    router0_b(loop)
                    for n in range(first_unit + 2, ROUND_UNITS * (loop + 1)):
                        max_of(n)
                    negated_maxima(loop)
                    e.wait_ge(w.za_ok, (E0 - DVE_SHARES) * (loop + 1))
                    e.wait_ge(w.cw_ok, loop + 1)
                    for ex in range(E0 - DVE_SHARES, E0):
                        for t in range(NT):
                            if ex > E0 - DVE_SHARES:
                                e.wait_ge(w.z_ok, NT * (DVE_SHARES * loop + ex - E0 + DVE_SHARES))
                            e.wait_ge(w.y_ps, (E0 + 1) * loop + ex + 1 + (t // (NT // 2) if ex == E0 - 1 else 0))
                            bank = last_bank(t) if ex == E0 - 1 else y_bank[ex % 2]
                            stt(z[:, t, :], bank[:, t * P:(t + 1) * P], cw[:, t, ex:ex + 1], z[:, t, :],
                                ALU.mult, ALU.add).then_inc(w.z_ok, 1)
                    e.wait_ge(w.z_ok, DVE_SHARES * NT * (loop + 1))
                    if loop == 0:
                        sum_squares(w.ssq_ok)
                        max_of(ROUND_UNITS)
                        e.wait_ge(w.rstd_ok, 1)
                        for t in range(NT):
                            ts(zs[:, t, :], z[:, t, :], rstd[:, t:t + 1], None, ALU.mult).then_inc(w.zs_ok, 1)
                for g in range(4):
                    e.wait_ge(w.pv_ps, NT * (g + 1))
                    if g:
                        e.wait_ge(w.oN_ps, g)
                    e.tensor_copy(o_sb[:, :], ps_u[:, g % 2, :]).then_inc(w.o_ok, 1)
                    e.wait_ge(w.oN_ps, g + 1)
                    src = ps_m[:, :].rearrange("p (a k) -> p a k", k=32)
                    link(e.reciprocal(oden[:, :, :], src[:, :, HD:HD + 1]))
                    dst = on[:, :, g, :].rearrange("p t (a v) -> p t a v", v=HD)
                    tt(dst, ps_m[:, :].rearrange("p (t a k) -> p t a k", t=NT, k=32)[:, :, :, 0:HD],
                       oden[:, :, 0].rearrange("p (t a) -> p t a", t=NT).unsqueeze(3).to_broadcast([P, NT, 4, HD]),
                       ALU.mult).then_inc(w.on_ok, 1)
                    if g == 0:
                        e.wait_ge(w.zc_ok, 1)
                        next_norms()
                flat = lambda v: v[:, :, :].rearrange("p t d -> p (t d)")
                x1f, xf, ynf, of, gf = flat(x1), flat(xin), flat(yn), flat(outb), flat(gate)
                e.wait_ge(w.att_ps, 1)
                e.wait_ge(w.gate_ok, 1)
                e.wait_ge(w.x_used, 1)
                link(tt(x1f, ps_y[:, :], gf, ALU.mult))
                tt(x1f, x1f, xf, ALU.add).then_inc(w.x1_ok, 1)
                e.wait_ge(w.x1_ok, 1)
                norm_stats(x1, bn6, mv, w.stats_ok)
                next_rest()
                e.wait_ge(w.rstd_ok, 2)
                for t in range(NT):
                    ts(yn[:, t, :], x1[:, t, :], mv[:, t, 0:1], rstd[:, t:t + 1], ALU.subtract, ALU.mult
                       ).then_inc(w.yn_ok, 1)

                next_v()
                split_x(LOOPS, w.xT_ok, w.hi_ok, w.lo_ok)
                e.wait_ge(w.lg_ps, LOOPS)
                ts(ld[:, :, 0:E1], ps_m[:, 0:NT * E1].rearrange("p (t x) -> p t x", t=NT), -1.0, None, ALU.mult
                   ).then_inc(w.sg_in, 1)
                e.wait_ge(w.tg_ok, 1)
                e.tensor_tensor_scan(acc[:, :], tg, ones_row[:, :], 0.0, ALU.add, ALU.add
                                     ).then_inc(w.acc_ok, 1)
                link(stt(wgt, tg, 1.0, xT[:, :], ALU.add, ALU.mult))
                tt(wc, wgt, cos_phi[:, :], ALU.mult)
                link(tt(ws[:, :], wgt, sin_phi[:, :], ALU.mult))
                e.wait_ge(w.mq_ps, 2)
                stt(phq, ps_u[:, 1, :], f_("b_q"), phi[:, :], ALU.add, ALU.add).then_inc(w.ph_ok, 1)
                e.wait_ge(w.ph_ok, 1)
                reduce_turns(link, phq, turns)
                ts(phq, phq, PI_BELOW, -PI_BELOW, ALU.min, ALU.max).then_inc(w.ph_ok, 1)

                def squared(i):
                    e.wait_ge(w.r_ok, i + 1)
                    tt(hid[:, i, :], hid[:, i, :], hid[:, i, :], ALU.mult).then_inc(w.a_ok, 1)

                e.tensor_tensor_scan(mem_r, ones_row[:, :], wc, 0.0, ALU.mult, ALU.add)
                link(e.tensor_tensor_scan(mem_i, ones_row[:, :], ws[:, :], 0.0, ALU.mult, ALU.add))
                e.wait_ge(w.inv_in, 1)
                link(e.reciprocal(inv[:, :], acc[:, :]))
                stt(mem_r, mem_r, MAG, inv[:, :], ALU.mult, ALU.mult).then_inc(w.mem_ok, 1)
                stt(mem_i, mem_i, MAG, inv[:, :], ALU.mult, ALU.mult).then_inc(w.mem_ok, 1)
                e.wait_ge(w.sc_ok, 2)
                e.wait_ge(w.mem_ok, 2)
                tt(turns, mem_i, sq, ALU.mult)
                e.wait_ge(w.sq_ok, 3)
                link(tt(mem_i, mem_i, cq, ALU.mult))
                e.wait_ge(w.rot_in, 2)
                tt(ctxt[:, 2, :], wc, turns, ALU.add).then_inc(w.ri_ok, 1)
                tt(ctxt[:, 3, :], mem_i, ws[:, :], ALU.subtract).then_inc(w.ri_ok, 1)
                e.wait_ge(w.sg_ok, 1)
                link(ts(le[:, :, 0:E1], le[:, :, 0:E1], 1.0, None, ALU.add))
                link(e.reciprocal(lg[:, :, 0:E1], le[:, :, 0:E1]))
                rk = rank_of(lg[:, :, 0:E1], E1, low8.unsqueeze(1).to_broadcast([P, NT, E1, E1]))
                link(stt(cw[:, :, :], rk, 1.5, lg[:, :, 0:E1], ALU.is_lt, ALU.mult))
                link(e.tensor_reduce(wsum[:, :], cw[:, :, :], AX.X, ALU.add))
                link(ts(wsum[:, :], wsum[:, :], 1e-20, None, ALU.add))
                link(e.reciprocal(wsum[:, :], wsum[:, :]))
                tt(cw[:, :, :], cw[:, :, :], bcast(wsum[:, :], E1), ALU.mult).then_inc(w.cw_ok, 1)
                squared(6)
                squared(7)
                e.wait_ge(w.g_ps, 1)
                link(e.tensor_copy(stat[:, :, :], ps_s[:, :, G1:G1 + 2]))
                link(tt(var[:, :], stat[:, :, 0], stat[:, :, 0], ALU.mult))
                tt(var[:, :], stat[:, :, 1], var[:, :], ALU.subtract).then_inc(w.var_ok, 1)
                e.wait_ge(w.rstd_ok, 3)
                for t in range(NT):
                    stt(ga[:, t, :], ps_s[:, t, 0:G1], rstd[:, t:t + 1], b1_all[:, :], ALU.mult, ALU.add
                        ).then_inc(w.ga_ok, 1)

                def share(ex):
                    if ex == ACT_SHARES:
                        e.wait_ge(w.za_ok, (E0 - DVE_SHARES) * LOOPS + ACT_SHARES - 1)
                        e.wait_ge(w.cw_ok, LOOPS + 1)
                    else:
                        e.wait_ge(w.share_ok, ex - ACT_SHARES)
                    e.wait_ge(w.y_ps, (E0 + 1) * LOOPS + ex + 1)
                    for t in range(NT):
                        i = stt(gate[:, t, :], y2_bank(ex)[:, t * P:(t + 1) * P], cw[:, t, ex:ex + 1],
                                gate[:, t, :], ALU.mult, ALU.add)
                    i.then_inc(w.share_ok, 1)

                share(4)
                split_x(1, w.head_xT_ok, w.head_hi_ok, w.head_lo_ok)
                for ex in range(5, E1):
                    share(ex)
                e.wait_ge(stored, 16)
                e.nop().then_inc(stored, -16)
                e.wait_ge(w.mlp_ps, 1)
                e.wait_ge(w.ynb_ok, 1)
                link(tt(of, ps_u[:, 1, :], ynf, ALU.add))
                e.wait_ge(w.gate_ok, 2)
                link(tt(of, of, gf, ALU.mult))
                tt(of, of, x1f, ALU.add).then_inc(w.out_ok, 1)
                meet(e, "dve")


_INPUTS = ("x", "first", "second", "w1", "w2", "v1", "v2", "rows")


def _layouts(i):
    a = {k: np.asarray(v) for k, v in i.items()}
    by_half = lambda v: v.reshape(2, HJ, D, HD).transpose(2, 0, 3, 1).reshape(D, D)
    column = lambda v: v.reshape(-1, P).T
    first = dict(
        ident=np.eye(P, dtype=np.float32),
        wq=by_half(a["L0_attn_W_query"]),
        wk=by_half(a["L0_attn_W_key"]),
        wv=a["L0_attn_W_val"].transpose(1, 0, 2).reshape(D, D),
        wr=np.concatenate([a["L0_ffn_w_macro"], a["L0_ffn_w_micro"].reshape(E0, D)]).T,
        norm_w=column(a["L0_ffn_norm_w"]),
        phases=column(a["L1_attn_random_phases"]),
        b_mag=column(a["L1_attn_b_mag"]),
        b_q=column(a["L1_attn_b_q"]),
        ln_g=column(a["L1_attn_ln_g"]),
        ln_b=column(a["L1_attn_ln_b"]),
        pos=np.broadcast_to(np.arange(S, dtype=np.float32), (P, S)),
    )
    return a, first, column


def kernel(**inputs):
    import concourse.bacc as bacc
    from concourse.bass_utils import run_bass_kernel_spmd as run

    a, first, column = _layouts(inputs)
    low = np.zeros((P, 2, 64), np.float32)
    low[:, 0, :16] = np.tril(np.ones((4, 4), np.float32), -1).ravel()
    low[:, 1, :] = np.tril(np.ones((8, 8), np.float32), -1).ravel()
    first["lower"] = low.reshape(P, 128)
    second = dict(
        wo=a["L0_attn_W_out"].reshape(2, 4, 2, HD, D).transpose(1, 0, 2, 3, 4).reshape(D, D),
        w_mag=a["L1_attn_W_mag"].T,
        w_q=a["L1_attn_W_q"].T,
        w2m=a["L1_attn_W2"].reshape(D, 2, P).transpose(2, 1, 0).reshape(P, G1),
        wr1=a["L1_ffn_router_w"].T,
        w1m=a["L1_attn_W1"].reshape(G1, CTX, P).transpose(2, 1, 0).reshape(P, CTX * G1),
    )
    arrays = dict(
        x=a["L0_attn_q"],
        first=np.concatenate([first[n] for n in FIRST], axis=1),
        second=np.concatenate([second[n] for n in SECOND], axis=1),
        w1=a["L0_ffn_w1"].reshape(E0 * F0, D).T,
        w2=a["L0_ffn_w2"].reshape(E0, D, 2, P).transpose(3, 0, 2, 1).reshape(P, C0 * D),
        v1=a["L1_ffn_w1"],
        v2=a["L1_ffn_w2"].reshape(E1, P, D).transpose(1, 0, 2).reshape(P, E1 * D),
        rows=np.concatenate([a["L1_attn_b1"], a["L1_attn_b2"]])[None, :],
    )
    nc = bacc.Bacc("TRN2", target_bir_lowering=False, num_devices=1)
    args, sent = [], {}
    for name in _INPUTS:
        v = np.ascontiguousarray(arrays[name])
        sent[f"in_{name}"] = v
        args.append(nc.dram_tensor(f"in_{name}", v.shape, mybir.dt.from_np(v.dtype), kind="ExternalInput").ap())
    args.append(nc.dram_tensor("out_0", (B, S, D), F32, kind="ExternalOutput").ap())
    build(nc, *args)
    return run(nc, [sent], core_ids=[0]).results[0]["out_0"]
```
